# Optimizing a Trainium2 kernel written in Bass

```python
import numpy as np
import jax
import jax.numpy as jnp

def _softmax(x, axis=-1):
    return jax.nn.softmax(x, axis=axis)

def _gelu(x):
    return jax.nn.gelu(x, approximate=True)

def _silu(x):
    return jax.nn.silu(x)

def _sigmoid(x):
    return jax.nn.sigmoid(x)

def _layernorm(x, axis=-1, eps=1e-05):
    m = jnp.mean(x, axis=axis, keepdims=True)
    v = jnp.var(x, axis=axis, keepdims=True)
    return (x - m) / jnp.sqrt(v + eps)

def _scatter_add(tgt, idx, src, axis=0):
    return tgt.at[idx].add(src)

def _segment_sum(src, seg, n):
    return jax.ops.segment_sum(src, seg, n)
kernel_name = 'mk_gnn_preln_d4_gnn_r8_1a58f6'

def setup_inputs(seed: int=0):
    np.random.seed(seed)
    _w = jnp.asarray

    def _rec_inputs():
        import jax
        import jax.numpy as jnp
        _gk = jax.random.key(seed)
        x = -6.415e-05 + 1 * jax.random.normal(jax.random.fold_in(_gk, 1), (1250, 512), jnp.float32)
        src = jax.random.randint(jax.random.fold_in(_gk, 2), (40000,), 0, 1250, jnp.int32)
        dst = jnp.minimum((1250 * jax.random.uniform(jax.random.fold_in(_gk, 3), (40000,)) ** 2.0).astype(jnp.int32), 9999)
        _o = jnp.argsort(dst, stable=True)
        src = src[_o]
        dst = dst[_o]
        edge_attr_20 = 0.000389844 + 1.00025 * jax.random.normal(jax.random.fold_in(_gk, 13), (40000, 20), jnp.float32)
        edge_attr_4 = -0.00185629 + 0.998788 * jax.random.normal(jax.random.fold_in(_gk, 14), (40000, 4), jnp.float32)
        edge_type_32 = jax.random.randint(jax.random.fold_in(_gk, 16), (40000,), 0, 32, jnp.int32)
        edge_weight = jax.random.uniform(jax.random.fold_in(_gk, 17), (40000,), jnp.float32, 0.0, 0.999993)
        edge_weight1 = jax.random.uniform(jax.random.fold_in(_gk, 18), (40000, 1), jnp.float32, 0.0, 0.999996)
        return (x, src, dst, edge_attr_20, edge_attr_4, edge_type_32, edge_weight, edge_weight1)
    x, src, dst, edge_attr_20, edge_attr_4, edge_type_32, edge_weight, edge_weight1 = _rec_inputs()

    def _L0_gnn_setup():
        import jax, jax.numpy as jnp
        import numpy as np
        N_NODES = 2500
        N_EDGES = 40000
        IN_FEAT = 512
        OUT_FEAT = 512
        NUM_RELS = 32
        NUM_BASES = 8
        key = jax.random.key(seed)
        ks = jax.random.split(key, 8)
        x = jax.random.normal(ks[0], (N_NODES, IN_FEAT), dtype=jnp.float32)
        bases = jax.random.normal(ks[1], (NUM_BASES, IN_FEAT, OUT_FEAT), dtype=jnp.float32) * (1.0 / np.sqrt(IN_FEAT))
        w_comp = jax.random.normal(ks[2], (NUM_RELS, NUM_BASES), dtype=jnp.float32) * (1.0 / np.sqrt(NUM_BASES))
        h_bias = jnp.zeros((OUT_FEAT,), dtype=jnp.float32)
        norm = jax.random.uniform(ks[3], (N_EDGES, 1), dtype=jnp.float32)
        src = jax.random.randint(ks[4], (N_EDGES,), 0, N_NODES, dtype=jnp.int32)
        dst = jax.random.randint(ks[5], (N_EDGES,), 0, N_NODES, dtype=jnp.int32)
        etype = jnp.sort(jax.random.randint(ks[6], (N_EDGES,), 0, NUM_RELS, dtype=jnp.int32))
        return {'x': x, 'bases': bases, 'w_comp': w_comp, 'h_bias': h_bias, 'norm': norm, 'src': src, 'dst': dst, 'etype': etype}
    _L0_gnn_all = _L0_gnn_setup()
    _L0_gnn_in = {k: v for k, v in _L0_gnn_all.items() if k in ('bases', 'w_comp', 'h_bias')}
    del _L0_gnn_all

    def _L1_gnn_setup():
        import jax, jax.numpy as jnp
        import numpy as np
        N_NODES = 1250

        def gcn_conv(x, edge_index, W, b):
            n = x.shape[0]
            h = x @ W
            loop = jnp.arange(n, dtype=edge_index.dtype)
            src = jnp.concatenate([edge_index[0], loop])
            dst = jnp.concatenate([edge_index[1], loop])
            ones = jnp.ones(src.shape[0], dtype=h.dtype)
            deg = jax.ops.segment_sum(ones, dst, num_segments=n)
            dis = jnp.where(deg > 0, jax.lax.rsqrt(deg), 0.0)
            norm = dis[src] * dis[dst]
            msg = h[src] * norm[:, None]
            out = jax.ops.segment_sum(msg, dst, num_segments=n)
            return out + b
        key = jax.random.key(seed)
        k1, k2, k3, k4, k5 = jax.random.split(key, 5)
        num_features, hidden, num_classes = (512, 512, 512)
        x = jax.random.normal(k1, (N_NODES, num_features), dtype=jnp.float32)
        edge_index = jax.random.randint(k2, (2, 20000), 0, N_NODES, dtype=jnp.int64)
        s1 = 1.0 / np.sqrt(num_features)
        s2 = 1.0 / np.sqrt(hidden)
        W1 = jax.random.uniform(k3, (num_features, hidden), jnp.float32, -s1, s1)
        b1 = jnp.zeros((hidden,), jnp.float32)
        W2 = jax.random.uniform(k4, (hidden, num_classes), jnp.float32, -s2, s2)
        b2 = jnp.zeros((num_classes,), jnp.float32)
        return {'x': x, 'edge_index': edge_index, 'W1': W1, 'b1': b1, 'W2': W2, 'b2': b2}
    _L1_gnn_all = _L1_gnn_setup()
    _L1_gnn_in = {k: v for k, v in _L1_gnn_all.items() if k in ('W1', 'b1', 'W2', 'b2')}
    del _L1_gnn_all

    def _L2_gnn_setup():
        import jax, jax.numpy as jnp
        import numpy as np
        import math
        B = 128
        F = 32
        R = 20
        N = 2048
        E = 32768
        LOG2 = 0.6931471805599453
        IS2 = 1.0 / math.sqrt(2.0)
        IS3 = 1.0 / math.sqrt(3.0)
        IS6 = 1.0 / math.sqrt(6.0)

        def ssp(x):
            return jax.nn.softplus(x) - LOG2
        key = jax.random.key(seed)
        ks = jax.random.split(key, 14)
        return dict(x=jax.random.normal(ks[0], (N, 4 * B), jnp.float32), idx_i=jax.random.randint(ks[1], (E,), 0, N), idx_j=jax.random.randint(ks[2], (E,), 0, N), f_ij=jax.random.normal(ks[3], (E, R), jnp.float32), rcut_ij=jax.random.uniform(ks[4], (E,), jnp.float32), Yr_ij=jax.random.normal(ks[5], (E, 4), jnp.float32), w_in2f_s=jax.random.normal(ks[6], (B, F), jnp.float32), w_in2f_v=jax.random.normal(ks[7], (B, F), jnp.float32), W1=jax.random.normal(ks[8], (R, F), jnp.float32) / math.sqrt(R), b1=jnp.zeros((F,), jnp.float32), W2=jax.random.normal(ks[9], (F, 6 * F), jnp.float32) / math.sqrt(F), b2=jnp.zeros((6 * F,), jnp.float32), w_f2o1_s=jax.random.normal(ks[10], (2 * F, B), jnp.float32), w_f2o1_v=jax.random.normal(ks[11], (2 * F, B), jnp.float32), w_f2o2_s=jax.random.normal(ks[12], (B, B), jnp.float32), w_f2o2_v=jax.random.normal(ks[13], (B, B), jnp.float32))
    _L2_gnn_all = _L2_gnn_setup()
    _L2_gnn_in = {k: v for k, v in _L2_gnn_all.items() if k in ('w_in2f_s', 'w_in2f_v', 'W1', 'b1', 'W2', 'b2', 'w_f2o1_s', 'w_f2o1_v', 'w_f2o2_s', 'w_f2o2_v')}
    del _L2_gnn_all

    def _L3_gnn_setup():
        import jax, jax.numpy as jnp
        import numpy as np
        N_NODES = 1250
        N_EDGES = 20000
        D_IN = 512
        D_HID = 512
        D_OUT = 512

        def _sage_conv(x, src, dst, W_l, W_r, b):
            n = x.shape[0]
            summed = jax.ops.segment_sum(x[src], dst, num_segments=n)
            deg = jax.ops.segment_sum(jnp.ones((src.shape[0],), x.dtype), dst, num_segments=n)
            agg = summed / jnp.maximum(deg, 1.0)[:, None]
            return agg @ W_l.T + x @ W_r.T + b
        key = jax.random.key(seed)
        ks = jax.random.split(key, 8)
        x = jax.random.normal(ks[0], (N_NODES, D_IN), dtype=jnp.float32)
        edge_index = jax.random.randint(ks[1], (2, N_EDGES), 0, N_NODES, dtype=jnp.int64)
        label = jax.random.randint(ks[2], (1,), 0, 3, dtype=jnp.int64)
        batch = jnp.zeros((N_NODES,), dtype=jnp.int64)
        s1 = 1.0 / np.sqrt(D_IN)
        s2 = 1.0 / np.sqrt(D_HID)
        W1_l = jax.random.normal(ks[3], (D_HID, D_IN), dtype=jnp.float32) * s1
        W1_r = jax.random.normal(ks[4], (D_HID, D_IN), dtype=jnp.float32) * s1
        b1 = jnp.zeros((D_HID,), dtype=jnp.float32)
        W2_l = jax.random.normal(ks[5], (D_OUT, D_HID), dtype=jnp.float32) * s2
        W2_r = jax.random.normal(ks[6], (D_OUT, D_HID), dtype=jnp.float32) * s2
        b2 = jnp.zeros((D_OUT,), dtype=jnp.float32)
        return {'x': x, 'label': label, 'edge_index': edge_index, 'batch': batch, 'W1_l': W1_l, 'W1_r': W1_r, 'b1': b1, 'W2_l': W2_l, 'W2_r': W2_r, 'b2': b2}
    _L3_gnn_all = _L3_gnn_setup()
    _L3_gnn_in = {k: v for k, v in _L3_gnn_all.items() if k in ('label', 'W1_l', 'W1_r', 'b1', 'W2_l', 'W2_r', 'b2')}
    del _L3_gnn_all
    return {'x': x, 'src': src, 'dst': dst, 'edge_attr_20': edge_attr_20, 'edge_attr_4': edge_attr_4, 'edge_type_32': edge_type_32, 'edge_weight': edge_weight, 'edge_weight1': edge_weight1, 'L0_gnn_bases': _L0_gnn_in['bases'], 'L0_gnn_w_comp': _L0_gnn_in['w_comp'], 'L0_gnn_h_bias': _L0_gnn_in['h_bias'], 'L1_gnn_W1': _L1_gnn_in['W1'], 'L1_gnn_b1': _L1_gnn_in['b1'], 'L1_gnn_W2': _L1_gnn_in['W2'], 'L1_gnn_b2': _L1_gnn_in['b2'], 'L2_gnn_w_in2f_s': _L2_gnn_in['w_in2f_s'], 'L2_gnn_w_in2f_v': _L2_gnn_in['w_in2f_v'], 'L2_gnn_W1': _L2_gnn_in['W1'], 'L2_gnn_b1': _L2_gnn_in['b1'], 'L2_gnn_W2': _L2_gnn_in['W2'], 'L2_gnn_b2': _L2_gnn_in['b2'], 'L2_gnn_w_f2o1_s': _L2_gnn_in['w_f2o1_s'], 'L2_gnn_w_f2o1_v': _L2_gnn_in['w_f2o1_v'], 'L2_gnn_w_f2o2_s': _L2_gnn_in['w_f2o2_s'], 'L2_gnn_w_f2o2_v': _L2_gnn_in['w_f2o2_v'], 'L3_gnn_label': _L3_gnn_in['label'], 'L3_gnn_W1_l': _L3_gnn_in['W1_l'], 'L3_gnn_W1_r': _L3_gnn_in['W1_r'], 'L3_gnn_b1': _L3_gnn_in['b1'], 'L3_gnn_W2_l': _L3_gnn_in['W2_l'], 'L3_gnn_W2_r': _L3_gnn_in['W2_r'], 'L3_gnn_b2': _L3_gnn_in['b2']}

def reference(x, src, dst, edge_attr_20, edge_attr_4, edge_type_32, edge_weight, edge_weight1, L0_gnn_bases, L0_gnn_w_comp, L0_gnn_h_bias, L1_gnn_W1, L1_gnn_b1, L1_gnn_W2, L1_gnn_b2, L2_gnn_w_in2f_s, L2_gnn_w_in2f_v, L2_gnn_W1, L2_gnn_b1, L2_gnn_W2, L2_gnn_b2, L2_gnn_w_f2o1_s, L2_gnn_w_f2o1_v, L2_gnn_w_f2o2_s, L2_gnn_w_f2o2_v, L3_gnn_label, L3_gnn_W1_l, L3_gnn_W1_r, L3_gnn_b1, L3_gnn_W2_l, L3_gnn_W2_r, L3_gnn_b2):
    import jax
    import jax.numpy as jnp

    def _L0_gnn_ref(x, bases, w_comp, h_bias, norm, src, dst, etype):
        import jax, jax.numpy as jnp
        import numpy as np
        N_NODES = 2500
        N_EDGES = 40000
        IN_FEAT = 512
        OUT_FEAT = 512
        NUM_RELS = 32
        NUM_BASES = 8
        n_nodes = x.shape[0]
        weight = jnp.einsum('rb,bio->rio', w_comp, bases)
        h_rel = jnp.einsum('ni,rio->rno', x, weight)
        msg = h_rel[etype, src] * norm
        out = jax.ops.segment_sum(msg, dst, num_segments=n_nodes)
        out = out + h_bias
        return out

    def _L1_gnn_ref(x, edge_index, W1, b1, W2, b2):
        import jax, jax.numpy as jnp
        import numpy as np
        N_NODES = 1250

        def gcn_conv(x, edge_index, W, b):
            n = x.shape[0]
            h = x @ W
            loop = jnp.arange(n, dtype=edge_index.dtype)
            src = jnp.concatenate([edge_index[0], loop])
            dst = jnp.concatenate([edge_index[1], loop])
            ones = jnp.ones(src.shape[0], dtype=h.dtype)
            deg = jax.ops.segment_sum(ones, dst, num_segments=n)
            dis = jnp.where(deg > 0, jax.lax.rsqrt(deg), 0.0)
            norm = dis[src] * dis[dst]
            msg = h[src] * norm[:, None]
            out = jax.ops.segment_sum(msg, dst, num_segments=n)
            return out + b
        h = jax.nn.relu(gcn_conv(x, edge_index, W1, b1))
        out = gcn_conv(h, edge_index, W2, b2)
        return out

    def _L2_gnn_ref(x, idx_i, idx_j, f_ij, rcut_ij, Yr_ij, w_in2f_s, w_in2f_v, W1, b1, W2, b2, w_f2o1_s, w_f2o1_v, w_f2o2_s, w_f2o2_v):
        import jax, jax.numpy as jnp
        import numpy as np
        import math
        B = 128
        F = 32
        R = 20
        N = 2048
        E = 32768
        LOG2 = 0.6931471805599453
        IS2 = 1.0 / math.sqrt(2.0)
        IS3 = 1.0 / math.sqrt(3.0)
        IS6 = 1.0 / math.sqrt(6.0)

        def ssp(x):
            return jax.nn.softplus(x) - LOG2
        n = x.shape[0]
        xs = x[:, :B]
        xv = x[:, B:].reshape(n, B, 3)
        hs = xs @ w_in2f_s / math.sqrt(B)
        hv = jnp.einsum('nbc,bf->nfc', xv, w_in2f_v) / math.sqrt(B)
        s = hs[idx_j]
        v = hv[idx_j]
        ys = Yr_ij[:, 0]
        yv = Yr_ij[:, 1:4]
        t_s1 = s * ys[:, None]
        t_s2 = jnp.einsum('efc,ec->ef', v, yv) * IS3
        t_v1 = s[:, :, None] * yv[:, None, :]
        t_v2 = v * ys[:, None, None]
        t_pv = jnp.cross(v, yv[:, None, :]) * IS2
        ax, ay, az = (v[..., 0], v[..., 1], v[..., 2])
        bx, by, bz = (yv[:, None, 0:1], yv[:, None, 1:2], yv[:, None, 2:3])
        bx, by, bz = (bx[..., 0], by[..., 0], bz[..., 0])
        t_q = jnp.stack([(ax * by + ay * bx) * IS2, (ay * bz + az * by) * IS2, (2.0 * az * bz - ax * bx - ay * by) * IS6, (ax * bz + az * bx) * IS2, (ax * bx - ay * by) * IS2], axis=-1)
        h = ssp(f_ij @ W1 + b1)
        Wij = (h @ W2 + b2) * rcut_ij[:, None]
        Wf = Wij.reshape(-1, F, 6)
        edge = jnp.concatenate([(t_s1 * Wf[..., 0])[..., None], (t_s2 * Wf[..., 1])[..., None], t_v1 * Wf[..., 2:3], t_v2 * Wf[..., 3:4], t_pv * Wf[..., 4:5], t_q * Wf[..., 5:6]], axis=-1)
        agg = jax.ops.segment_sum(edge.reshape(edge.shape[0], -1), idx_i, num_segments=n).reshape(n, F, 16)
        s_in = jnp.concatenate([agg[..., 0], agg[..., 1]], axis=1)
        v_in = jnp.concatenate([agg[..., 2:5], agg[..., 5:8]], axis=1)
        os1 = s_in @ w_f2o1_s / math.sqrt(2 * F)
        ov1 = jnp.einsum('nmc,mb->nbc', v_in, w_f2o1_v) / math.sqrt(2 * F)
        os1 = ssp(os1)
        os2 = os1 @ w_f2o2_s / math.sqrt(B)
        ov2 = jnp.einsum('nbc,bd->ndc', ov1, w_f2o2_v) / math.sqrt(B)
        return jnp.concatenate([os2, ov2.reshape(n, -1)], axis=-1)

    def _L3_gnn_ref(x, label, edge_index, batch, W1_l, W1_r, b1, W2_l, W2_r, b2):
        import jax, jax.numpy as jnp
        import numpy as np
        N_NODES = 1250
        N_EDGES = 20000
        D_IN = 512
        D_HID = 512
        D_OUT = 512

        def _sage_conv(x, src, dst, W_l, W_r, b):
            n = x.shape[0]
            summed = jax.ops.segment_sum(x[src], dst, num_segments=n)
            deg = jax.ops.segment_sum(jnp.ones((src.shape[0],), x.dtype), dst, num_segments=n)
            agg = summed / jnp.maximum(deg, 1.0)[:, None]
            return agg @ W_l.T + x @ W_r.T + b
        src, dst = (edge_index[0], edge_index[1])
        h = _sage_conv(x, src, dst, W1_l, W1_r, b1)
        h = jnp.tanh(h)
        out = _sage_conv(h, src, dst, W2_l, W2_r, b2)
        return out
    edge_index = jnp.stack([src, dst])
    batch0 = jnp.zeros((1250,), jnp.int32)
    h = jnp.maximum(_layernorm(x, axis=-1), 0.0)
    x = x + _L0_gnn_ref(h, L0_gnn_bases, L0_gnn_w_comp, L0_gnn_h_bias, edge_weight1, src, dst, edge_type_32)
    h = jnp.maximum(_layernorm(x, axis=-1), 0.0)
    x = x + _L1_gnn_ref(h, edge_index, L1_gnn_W1, L1_gnn_b1, L1_gnn_W2, L1_gnn_b2)
    h = jnp.maximum(_layernorm(x, axis=-1), 0.0)
    x = x + _L2_gnn_ref(h, src, dst, edge_attr_20, edge_weight, edge_attr_4, L2_gnn_w_in2f_s, L2_gnn_w_in2f_v, L2_gnn_W1, L2_gnn_b1, L2_gnn_W2, L2_gnn_b2, L2_gnn_w_f2o1_s, L2_gnn_w_f2o1_v, L2_gnn_w_f2o2_s, L2_gnn_w_f2o2_v)
    h = jnp.maximum(_layernorm(x, axis=-1), 0.0)
    x = x + _L3_gnn_ref(h, L3_gnn_label, edge_index, batch0, L3_gnn_W1_l, L3_gnn_W1_r, L3_gnn_b1, L3_gnn_W2_l, L3_gnn_W2_r, L3_gnn_b2)
    return x

_drawn_inputs = setup_inputs


def setup_inputs(seed=0):
    import zlib

    import numpy as np

    out = dict(_drawn_inputs(seed))
    spreads = {'L0_gnn_h_bias': (0.0, 0.1),
     'L1_gnn_b1': (0.0, 0.569),
     'L1_gnn_b2': (0.0, 0.1),
     'L2_gnn_b1': (0.0, 0.337),
     'L2_gnn_b2': (0.0, 0.1),
     'L3_gnn_b1': (0.0, 0.289),
     'L3_gnn_b2': (0.0, 0.292)}
    factors = {}
    for name, (base, spread) in spreads.items():
        noise = np.random.default_rng([zlib.crc32(name.encode()), seed]).standard_normal(out[name].shape)
        drawn = base * np.exp(spread * noise) if base else spread * noise
        out[name] = jnp.asarray(drawn.astype(out[name].dtype))
    for name, factor in factors.items():
        out[name] = (out[name] * factor).astype(out[name].dtype)
    return out
```

```python
import concourse.bass as bass
from concourse import mybir
from contextlib import ExitStack

P = 128
NODES, FEAT, EDGES = 1250, 512, 40000
BLOCKS = -(-NODES // P)
LAST = NODES - (BLOCKS - 1) * P
KIN = FEAT // P
CHUNKS = 320
REAL_CHUNKS = -(-EDGES // P)
TAIL = EDGES - (REAL_CHUNKS - 1) * P
BASES, RELS = 8, 32
WIN = 16
WINDOWS = -(-NODES // WIN)
DSTP = WINDOWS * WIN
AWIN = WIN * BLOCKS
RING = 8
QUAD = 4
GROUP = 2 * P
STEPS = 84
GROUPS = 2 * STEPS
SLOTS = GROUPS * GROUP
ROW = 32
YCOL, RCUT, DSTC, SRCC = 20, 24, 25, 26
RAD, HID = 20, 32
MSG = 320
PADDST = 4096
LOG2 = 0.6931471805599453
IS3 = 3.0 ** -0.5
EPS = 1e-5
COLS = [(0, 417), (417, 834), (834, 1250)]
ETS = 8
SLICES = CHUNKS // QUAD // ETS
assert EDGES // GROUP + BLOCKS <= GROUPS


def rows(n):
    return P if n < BLOCKS - 1 else LAST


class Count:

    def __init__(self):
        self.n = 0

    def up(self):
        self.n = self.n + 1
        return 1


def graph_layers(nc, src, dst, etype, norm, attr, x, bases, w_comp, h_bias, g_w1, g_b1, g_w2, g_b2,
                 m_ws, m_wv, m_w1, m_b1, m_w2, m_b2, m_os, m_ov, m_qs, m_qv,
                 s_w1l, s_w1r, s_b1, s_w2l, s_w2r, s_b2, out):
    f32, f16, bf16 = mybir.dt.float32, mybir.dt.float16, mybir.dt.bfloat16
    i32, u16 = mybir.dt.int32, mybir.dt.uint16
    ALU, ACT = mybir.AluOpType, mybir.ActivationFunctionType

    h_rows = nc.dram_tensor("h_rows", (NODES, FEAT), f32).ap()
    x1_rows = nc.dram_tensor("x1_rows", (NODES, FEAT), f32).ap()
    slots = nc.dram_tensor("slots", (SLOTS, ROW), f32).ap()
    u_rows = nc.dram_tensor("u_rows", (NODES, P), f32).ap()

    ctx = ExitStack()
    with ctx:
        def sb(scope, name, shape, dt):
            return scope.enter_context(nc.sbuf_tensor(name, shape, dt))

        def sem(name):
            return ctx.enter_context(nc.semaphore(name))

        ident = sb(ctx, "ident", [P, P], f32)
        ones = sb(ctx, "ones", [P, P], f32)
        below = sb(ctx, "below", [P, P], bf16)
        ones_b = sb(ctx, "ones_b", [P, P], bf16)
        iota_a = sb(ctx, "iota_a", [P, AWIN], f16)
        src_i = sb(ctx, "src_i", [P, CHUNKS], i32)
        dst_i = sb(ctx, "dst_i", [P, CHUNKS], i32)
        acol = sb(ctx, "acol", [P, CHUNKS], f16)
        srclo = sb(ctx, "srclo", [P, CHUNKS], f16)
        win_i = sb(ctx, "win_i", [1, CHUNKS], i32)
        slot_i = sb(ctx, "slot_i", [P, CHUNKS], i32)
        fits = sb(ctx, "fits", [1, 1], i32)
        start_k = sb(ctx, "start_k", [P, BLOCKS + 1], f32)
        idx_s = sb(ctx, "idx_s", [P, 2, QUAD], i32)
        stat6 = sb(ctx, "stat6", [P, BLOCKS, 6], f32)
        mv = sb(ctx, "mv", [P, BLOCKS, 2], f32)
        std = sb(ctx, "std", [P, BLOCKS], f32)
        rstd = sb(ctx, "rstd", [P, BLOCKS], f32)
        nmr = sb(ctx, "nmr", [P, BLOCKS], f32)
        epsb = sb(ctx, "epsb", [P, 1], f32)
        iota_w = sb(ctx, "iota_w", [P, WIN], f32)
        sized_i = sb(ctx, "sized_i", [P, 2], i32)
        one_off = sb(ctx, "one_off", [P, 2], f32)
        turn = sb(ctx, "turn", [P, 2], f32)

        z_scope = ExitStack()
        z = sb(z_scope, "z", [P, KIN, BASES, DSTP], f32)
        zk = [z[:, k, :, :].rearrange("p b d -> p (b d)") for k in range(KIN)]
        x_in = zk[KIN - 1][:, 0:BLOCKS * FEAT].rearrange("p (n f) -> p n f", f=FEAT)
        coef_scope = ExitStack()
        coef = sb(coef_scope, "coef", [P, CHUNKS, BASES], f32)
        offs = sb(coef_scope, "offs", [P, CHUNKS], f16)
        part = ExitStack()
        et_i = sb(part, "et_i", [P, 2, ETS * P], i32)
        et_1 = sb(part, "et_1", [P, 2, ETS * P], f32)
        norm_f = sb(part, "norm_f", [P, CHUNKS], f32)
        wc_blk = sb(part, "wc_blk", [P, QUAD * BASES], f32)
        rel_id = sb(part, "rel_id", [P, 1], f32)
        pid = sb(part, "pid", [P, 1], f32)
        pid_i = sb(part, "pid_i", [P, 2], i32)
        col_id = sb(part, "col_id", [P, P], f32)
        win_f = sb(part, "win_f", [1, CHUNKS], f32)
        tmp_a = sb(part, "tmp_a", [P, CHUNKS], f32)
        tmp_b = sb(part, "tmp_b", [P, CHUNKS], f32)
        tmp_i = sb(part, "tmp_i", [P, CHUNKS], i32)
        inside = sb(part, "inside", [P, 1], f32)
        part.close()
        part = ExitStack()
        gath = sb(part, "gath", [P, RING, FEAT], f32)
        idx = sb(part, "idx", [P, 4, QUAD], i32)
        spread = sb(part, "spread", [P, 2, QUAD, BASES, WIN], f32)
        hit = sb(part, "hit", [P, 2, QUAD, WIN], f32)
        part.close()
        coef_scope.close()
        part = ExitStack()
        cnt = sb(part, "cnt", [P, BLOCKS, DSTP], u16)
        base_t = sb(part, "base_t", [P, KIN, FEAT], f32)
        xt = sb(part, "xt", [P, 2, FEAT], f32)
        hot_s = sb(part, "hot_s", [P, 2, P], f16)
        hot_d = sb(part, "hot_d", [P, 2, AWIN], f16)
        att = sb(part, "att", [P, 2, QUAD, ROW], f32)
        bias0 = sb(part, "bias0", [P, FEAT], f32)
        part.close()
        z_scope.close()
        run_sum = xt[:, 0, 0:CHUNKS]
        place = xt[:, 1, 0:CHUNKS]
        in_blk = xt[:, 0, CHUNKS:CHUNKS + CHUNKS // 2].bitcast(bf16)
        blk_f = base_t[:, 3, 0:CHUNKS]
        blk_i = base_t[:, 0, 0:CHUNKS].bitcast(i32)
        slot_f = base_t[:, 1, 0:CHUNKS]

        late = ExitStack()
        adj = sb(late, "adj", [P, BLOCKS, NODES], f32)
        xs = sb(late, "xs", [P, BLOCKS, FEAT], f32)
        hs = sb(late, "hs", [P, BLOCKS, FEAT], f32)
        gt = sb(late, "gt", [P, KIN, NODES], f32)
        ht = sb(late, "ht", [P, KIN, NODES], f32)
        wa = sb(late, "wa", [P, KIN, FEAT], f32)
        wb = sb(late, "wb", [P, KIN, FEAT], f32)
        b_a = sb(late, "b_a", [P, FEAT], f32)
        b_b = sb(late, "b_b", [P, FEAT], f32)
        low = sb(late, "low", [P, 2, FEAT], f32)
        deg = sb(late, "deg", [P, BLOCKS], f32)
        dis = sb(late, "dis", [P, BLOCKS], f32)
        inv = sb(late, "inv", [P, BLOCKS], f32)
        seg_i = sb(late, "seg_i", [1, GROUPS], i32)
        seg_f = sb(late, "seg_f", [1, GROUPS], f32)
        seg_g = sb(late, "seg_g", [1, GROUPS], f32)
        at = sb(late, "at", [P, 2, QUAD, 2, 2 * ROW], f32)
        u = sb(late, "u", [P, QUAD, QUAD, P], f32)
        ey = sb(late, "ey", [P, 2, QUAD, 3, 2 * HID], f32)
        py = sb(late, "py", [P, 2, QUAD, 2 * HID], f32)
        msg = sb(late, "msg", [P, 2, QUAD, MSG], f32)
        hot = sb(late, "hot", [P, 2, QUAD, P], f32)
        yr = sb(late, "yr", [P, 4, QUAD, 4], f32)
        at_t = sb(late, "at_t", [P, 2, P], f32)
        soft = sb(late, "soft", [P, 2, 3, P], f32)
        hid = sb(late, "hid", [P, 2, P], f32)
        iota_h = sb(late, "iota_h", [P, P], f32)
        w1_blk = sb(late, "w1_blk", [P, P], f32)
        w2_blk = sb(late, "w2_blk", [P, QUAD * P], f32)
        b1_c = sb(late, "b1_c", [P, 1], f32)
        b2_f = sb(late, "b2_f", [1, 2, P], f32)
        b2_r = sb(late, "b2_r", [1, 3, P], bf16)
        ws_t = sb(late, "ws_t", [P, HID], f32)
        wv_t = sb(late, "wv_t", [P, HID], f32)
        late.close()
        agg = gt[:, :, :].rearrange("p k n -> p (k n)")[:, 0:BLOCKS * MSG]
        flat = ht[:, :, :].rearrange("p k n -> p (k n)")
        os_t, ov_t, qs_t, qv_t = (flat[:, P * i:P * (i + 1)] for i in range(4))
        agg_t = flat[:, 4 * P:10 * P].rearrange("p (a j n) -> p a j n", a=2, j=3)
        sv_t = flat[:, 10 * P:18 * P].rearrange("p (a j n) -> p a j n", a=2, j=4)
        ssp = flat[:, 18 * P:24 * P].rearrange("p (a j n) -> p a j n", a=2, j=3)

        ps = [ctx.enter_context(nc.psum_tensor(f"ps{i}", [P, 512], f32)) for i in range(8)]

        def semaphores(names):
            return [sem(n) for n in names.split()]

        ld_tab, ld_wc, ld_bias, st_h, st_zero, ld_w12, ld_w2b, st_out, st_u, ld_mp, ld_mq, ld_x1 = semaphores(
            "ld_tab ld_wc ld_bias st_h st_zero ld_w12 ld_w2b st_out st_u ld_mp ld_mq ld_x1")
        ld_x = semaphores("ld_x0 ld_x1a ld_x2")
        ld_et = semaphores("ld_et0 ld_et1")
        ld_base = semaphores("ld_base0 ld_base1 ld_base2 ld_base3")
        ld_xt, st_xt = semaphores("ld_xt0 ld_xt1"), semaphores("st_xt0 st_xt1")
        ld_att, st_att = semaphores("ld_att0 ld_att1"), semaphores("st_att0 st_att1")
        ld_at = semaphores("ld_at0 ld_at1")
        st_o = semaphores("st_o0 st_o1")
        gathered = [sem(f"gathered{i}") for i in range(RING)]
        u_in = [sem(f"u_in{i}") for i in range(QUAD)]
        const, cnt_in, hit_ok, g_o, ga_o, z_zero, z_zero_a, et_hot, win_out, win_pe, cnt_pe, coef_pe, coef_ok, fit_ok = semaphores(
            "const cnt_in hit_ok g_o ga_o z_zero z_zero_a et_hot win_out win_pe cnt_pe coef_pe coef_ok fit_ok")
        ln_stat, ln_std, ln_rs, ln_h = semaphores("ln_stat ln_std ln_rs ln_h")
        idx_ok, spread_ok, z_pe, z_add = semaphores("idx_ok spread_ok z_pe z_add")
        g_idx, g_gath, g_spread, g_pe, g_add, edges_done = semaphores(
            "g_idx g_gath g_spread g_pe g_add edges_done")
        in_ok, rank_pe, rank_ok, cnt_zero = semaphores("in_ok rank_pe rank_ok cnt_zero")
        hot_ok, a_pe, a_add, ga_hot, ga_pe, ga_add, cnt_done = semaphores(
            "hot_ok a_pe a_add ga_hot ga_pe ga_add cnt_done")
        tile_pe, half_pe, o_free, o_done, att_ok = semaphores(
            "tile_pe half_pe o_free o_done att_ok")
        adj_act, adj_ok, deg_pe, deg_ok, deg_sq, agg_pe, gt_ok, lin_pe, lin_ok, act_h = semaphores(
            "adj_act adj_ok deg_pe deg_ok deg_sq agg_pe gt_ok lin_pe lin_ok act_h")
        u_pe, u_ev, t_pe, t_act, h_pe, h_act, h_ok, w_pe, e_ok, y_ok, p_ok, m_ok, m_pe, m_add, pre_ok = semaphores(
            "u_pe u_ev t_pe t_act h_pe h_act h_ok w_pe e_ok y_ok p_ok m_ok m_pe m_add pre_ok")
        q_t, q_ev, q_o, q_act, q_ok, q_pe, q_x = semaphores("q_t q_ev q_o q_act q_ok q_pe q_x")
        dve_o, act_o = semaphores("dve_o act_o")

        ld_w3, ld_w4 = semaphores("ld_w3 ld_w4")
        REAL_QUADS = -(-REAL_CHUNKS // QUAD)
        ATT_DONE = [16 * len([t for t in range(REAL_CHUNKS) if t // QUAD % 2 == par]) for par in range(2)]

        def steps(eng, n, first, last, body, skip=0):
            for i in range(skip, first):
                body(i)
            with eng.Fori(first, n - last) as i:
                body(i)
            for i in range(n - last, n):
                body(i)

        def valid(st):
            return not isinstance(st, int) or 0 <= st < STEPS

        def message_steps(eng, body):
            for st in range(-3, 8):
                body(st, st % 2, st % 8)
            with eng.Fori(1, STEPS // 8) as i:
                for s8 in range(8):
                    body(i * 8 + s8, s8 % 2, s8)
            for st in range(STEPS // 8 * 8, STEPS):
                body(st, st % 2, st % 8)

        def lap16(st, s):
            return 2 * (st - s) + 16 * (s // 8) + 16

        def in_reg(eng, value):
            return value if isinstance(value, int) else eng.to_reg(value)

        def after(eng, s, value):
            if not isinstance(value, int) or value > 0:
                eng.wait_ge(s, value)

        block = ctx.enter_context(nc.Block())

        @block.sync
        def _(sp):
            sp.dma_start(dst_i[:, :], dst).then_inc(ld_tab, 16)
            sp.dma_start(src_i[:, :], src).then_inc(ld_tab, 16)
            sp.dma_start(norm_f[:, :], norm).then_inc(ld_tab, 16)
            for s, (a, b) in zip(ld_x, ((0, 4), (4, 9))):
                sp.dma_start(x_in[:, a:b, :], x[a * P:b * P, :].rearrange("(n p) f -> p n f", p=P)).then_inc(s, 16)
            sp.dma_start(x_in[0:LAST, 9, :], x[9 * P:NODES, :]).then_inc(ld_x[2], 16)
            sp.wait_ge(const, 1)
            for q in range(QUAD):
                sp.dma_start(wc_blk[RELS * q:RELS * (q + 1), BASES * q:BASES * (q + 1)], w_comp).then_inc(ld_wc, 16)
            for j in range(CHUNKS // QUAD // ETS):
                if j >= 2:
                    sp.wait_ge(et_hot, j - 1)
                for q in range(QUAD):
                    sp.dma_start(et_i[RELS * q:RELS * (q + 1), j % 2, :],
                                 etype[q:q + 1, j * ETS * P:(j + 1) * ETS * P].to_broadcast([RELS, ETS * P]))\
                        .then_inc(ld_et[j % 2], 16)
            for n in range(BLOCKS):
                sp.wait_ge(ln_h, n + 1)
                sp.dma_start(h_rows[n * P:n * P + rows(n), :], x_in[0:rows(n), n, :]).then_inc(st_h, 16)
            sp.wait_ge(z_zero, 1)
            per = SLOTS * ROW // P // 2
            for i in range(2):
                sp.dma_start(slots[i * SLOTS // 2:(i + 1) * SLOTS // 2, :].rearrange("(p a) c -> p (a c)", p=P),
                             zk[0][:, 0:per]).then_inc(st_zero, 16)
            sp.wait_ge(edges_done, 1)

            def attributes(g, par, lap):
                after(sp, st_att[par], 16 * QUAD * lap)
                sp.dma_start(att[:, par, :, :], attr[:, bass.ds(g * QUAD, QUAD), :]).then_inc(ld_att[par], 16)

            def attribute_pair(i):
                for par in range(2):
                    attributes(2 * i + par, par, i)

            steps(sp, REAL_QUADS // 2, 1, 0, attribute_pair)
            attributes(REAL_QUADS - 1, (REAL_QUADS - 1) % 2, REAL_QUADS // 2)
            sp.wait_ge(adj_ok, 1)
            for par in range(2):
                sp.wait_ge(st_att[par], ATT_DONE[par])
            sp.wait_ge(cnt_zero, 2)
            for c in range(QUAD):
                h = slice(HID * c, HID * (c + 1))
                sp.dma_start(w1_blk[HID * c:HID * c + RAD, h], m_w1).then_inc(ld_mp, 16)
                sp.dma_start(w2_blk[h, P * c:P * (c + 1)], m_w2).then_inc(ld_mp, 16)
                sp.dma_start(b1_c[h, :], m_b1).then_inc(ld_mp, 16)
            sp.dma_start(b2_f[0:1, 0, :], m_b2).then_inc(ld_mp, 16)
            sp.dma_start(ws_t[:, :], m_ws).then_inc(ld_mp, 16)
            sp.dma_start(wv_t[:, :], m_wv).then_inc(ld_mp, 16)

            def sorted_quad(qn, par):
                after(sp, m_ok, QUAD * (qn - 1))
                sp.dma_start(at[:, par, :, :, :].rearrange("p s g w -> p (s g) w"),
                             slots[bass.ds(qn * QUAD * 2 * GROUP, QUAD * 2 * GROUP), :].rearrange(
                                 "(s p c) w -> p s (c w)", p=P, c=2)).then_inc(ld_at[par], 16)

            for qn in range(2):
                sorted_quad(qn, qn)
            sp.wait_ge(u_ev, BLOCKS)
            for i in range(QUAD):
                a = min(i, 1)
                sp.dma_start(os_t[HID * i:HID * (i + 1), :], m_os[HID * a:HID * (a + 1), :]).then_inc(ld_mq, 16)
            for i in range(2):
                sp.dma_start(ov_t[2 * HID * i:2 * HID * (i + 1), :], m_ov).then_inc(ld_mq, 16)
            sp.dma_start(qs_t, m_qs).then_inc(ld_mq, 16)
            sp.dma_start(qv_t, m_qv).then_inc(ld_mq, 16)
            sp.wait_ge(lin_ok, 2 * BLOCKS)
            for t, w in ((wa, s_w1l), (wb, s_w1r)):
                sp.dma_start(t[:, :, :], w.rearrange("(k p) f -> p k f", p=P)).then_inc(ld_w3, 16)
            for t, w in ((b_a, s_b1), (b_b, s_b2)):
                sp.dma_start(t[:, :], w.to_broadcast([P, FEAT])).then_inc(ld_w3, 16)

            def sorted_pair(i):
                for par in range(2):
                    sorted_quad(2 * i + par, par)

            steps(sp, STEPS // QUAD // 2, 1, 0, sorted_pair, skip=1)
            sorted_quad(STEPS // QUAD - 1, 0)
            sp.wait_ge(lin_ok, 4 * BLOCKS)
            for t, w in ((wa, s_w2l), (wb, s_w2r)):
                sp.dma_start(t[:, :, :], w.rearrange("(k p) f -> p k f", p=P)).then_inc(ld_w4, 16)
            for n in range(BLOCKS):
                sp.wait_ge(lin_ok, 4 * BLOCKS + 2 * (n + 1))
                sp.dma_start(out[n * P:n * P + rows(n), :], low[0:rows(n), n % 2, :]).then_inc(st_o[n % 2], 16)
            for par in range(2):
                sp.wait_ge(st_o[par], 16 * BLOCKS // 2)

        @block.scalar
        def _(act):
            def ln_std_of(k, n):
                r = rows(n)
                act.wait_ge(ln_stat, BLOCKS * k + n + 1)
                nc.scalar.activation(std[0:r, n:n + 1], mv[0:r, n, 1:2], ACT.Sqrt, bias=epsb[0:r, :]).then_inc(ln_std, 1)

            def ln_h_of(k, n, src_t, dst_t):
                r = rows(n)
                act.wait_ge(ln_rs, BLOCKS * k + n + 1)
                nc.scalar.activation(dst_t[0:r, n, :], src_t[0:r, n, :], ACT.Relu, bias=nmr[0:r, n:n + 1],
                                     scale=rstd[0:r, n:n + 1]).then_inc(ln_h, 1)

            def layernorm(k, src_t, dst_t):
                for n in range(BLOCKS + 1):
                    if n < BLOCKS:
                        ln_std_of(k, n)
                    if n:
                        ln_h_of(k, n - 1, src_t, dst_t)

            act.wait_ge(const, 1)
            layernorm(0, x_in, x_in)
            act.wait_ge(z_zero, 1)
            nc.scalar.activation(zk[2], zk[0], ACT.Copy).then_inc(z_zero_a, 1)
            act.wait_ge(st_h, 16 * BLOCKS)
            nc.scalar.activation(zk[3], zk[0], ACT.Copy).then_inc(z_zero_a, 1)
            act.wait_ge(edges_done, 1)
            act.dma_start(bias0[:, :], h_bias.to_broadcast([P, FEAT])).then_inc(ld_bias, 16)
            act.wait_ge(rank_ok, 1)

            def x_tile(m):
                if m >= 2:
                    act.wait_ge(st_xt[m % 2], 16 * (m // 2))
                act.dma_start(xt[0:rows(m), m % 2, :], x[m * P:m * P + rows(m), :]).then_inc(ld_xt[m % 2], 16)

            for m in range(2):
                x_tile(m)
            for half in range(2):
                for b in range(BASES):
                    for k in range(KIN):
                        use = half * BASES + b
                        if use:
                            act.wait_ge(tile_pe, (use - 1) * KIN + k + 1)
                        act.dma_start(base_t[:, k, :], bases[b, k * P:(k + 1) * P, :]).then_inc(ld_base[k], 16)
                for m in range(5 * half, 5 * half + 5):
                    act.wait_ge(o_done, m + 1)
                    act.dma_start(x1_rows[m * P:m * P + rows(m), :], xt[0:rows(m), m % 2, :]).then_inc(st_xt[m % 2], 16)
                    if m + 2 < BLOCKS:
                        x_tile(m + 2)
            for m in range(2):
                act.wait_ge(st_xt[m], 16 * BLOCKS // 2)
            act.dma_start(xs[:, 0:9, :], x1_rows[0:9 * P, :].rearrange("(n p) f -> p n f", p=P)).then_inc(ld_x1, 16)
            act.dma_start(xs[0:LAST, 9, :], x1_rows[9 * P:NODES, :]).then_inc(ld_x1, 16)
            for t, w in ((wa, g_w1), (wb, g_w2)):
                act.dma_start(t[:, :, :], w.rearrange("(k p) f -> p k f", p=P)).then_inc(ld_w12, 16)
            for t, w in ((b_a, g_b1), (b_b, g_b2)):
                act.dma_start(t[:, :], w.to_broadcast([P, FEAT])).then_inc(ld_w12, 16)
            act.wait_ge(half_pe, 2)
            act.wait_ge(cnt_done, 1)
            for s in range(5, BLOCKS):
                nc.scalar.activation(adj[:, s, :], cnt[:, s, 0:NODES], ACT.Copy).then_inc(adj_act, 1)
            act.wait_ge(deg_ok, 1)
            nc.scalar.activation(dis[:, :], deg[:, :], ACT.Sqrt).then_inc(deg_sq, 1)
            layernorm(1, xs, hs)

            n_agg, n_gt, n_h = Count(), Count(), Count()

            def evacuate_transposed(r, n):
                act.wait_ge(agg_pe, n_agg.n + 1)
                bank = ps[n_agg.n % 4]
                n_agg.up()
                nc.scalar.activation(ht[:, :, n * P:n * P + r],
                                     bank[:, :].rearrange("p (k c) -> p k c", k=KIN)[:, :, 0:r], ACT.Copy)\
                    .then_inc(gt_ok, n_gt.up())

            def evacuate_aggregated():
                for a, b in COLS:
                    for k in range(KIN):
                        act.wait_ge(agg_pe, n_agg.n + 1)
                        bank = ps[n_agg.n % 4]
                        n_agg.up()
                        nc.scalar.activation(gt[:, k, a:b], bank[:, 0:b - a], ACT.Copy).then_inc(gt_ok, n_gt.up())

            evacuate_aggregated()
            for n in range(BLOCKS):
                r = rows(n)
                act.wait_ge(lin_ok, n + 1)
                nc.scalar.activation(hs[0:r, n, :], low[0:r, n % 2, :], ACT.Relu, scale=dis[0:r, n:n + 1])\
                    .then_inc(act_h, n_h.up())
            evacuate_aggregated()
            layernorm(2, xs, hs)
            scale_b = P ** -0.5
            for n in range(BLOCKS + 1):
                if n < BLOCKS:
                    evacuate_transposed(rows(n), n)
                if n:
                    r = rows(n - 1)
                    act.wait_ge(u_pe, n)
                    nc.scalar.activation(u[0:r, (n - 1) // 4, (n - 1) % 4, :], ps[4 + (n - 1) % 2][0:r, 0:P], ACT.Copy,
                                         scale=scale_b).then_inc(u_ev, 1)
                    act.wait_ge(u_ev, n)
                    act.dma_start(u_rows[(n - 1) * P:(n - 1) * P + r, :], u[0:r, (n - 1) // 4, (n - 1) % 4, :])\
                        .then_inc(st_u, 16)

            def radial(st, par, s8):
                if valid(st + 3):
                    act.wait_ge(t_pe, st + 4)
                    after(act, h_pe, st + 2)
                    nc.scalar.activation(at_t[:, 1 - par, :], ps[2][:, 0:P], ACT.Copy).then_inc(t_act, 1)
                if valid(st + 2):
                    act.wait_ge(h_pe, st + 3)
                    after(act, h_ok, st + 1)
                    nc.scalar.activation(soft[:, par, 0, :], ps[3][:, 0:P], ACT.Abs, bias=b1_c[:, :]).then_inc(act_o, 1)
                    nc.scalar.activation(soft[:, par, 2, :], ps[3][:, 0:P], ACT.Relu, bias=b1_c[:, :]).then_inc(h_act, 1)
                    act.wait_ge(act_o, 2 * (st + 2) + 1)
                    nc.scalar.activation(soft[:, par, 1, :], soft[:, par, 0, :], ACT.Exp, scale=-1.0).then_inc(act_o, 1)
                    act.wait_ge(act_o, 2 * (st + 2) + 2)
                    nc.scalar.activation(soft[:, par, 0, :], soft[:, par, 1, :], ACT.Ln, bias=1.0).then_inc(h_act, 1)
                if valid(st + 1):
                    act.wait_ge(w_pe, st + 2)
                    act.wait_ge(y_ok, st + 2)
                    after(act, m_ok, st)
                    for c in range(QUAD):
                        for y in range(3):
                            last = nc.scalar.activation(ey[:, 1 - par, c, y, :], ps[1 - par][:, c * P + 64:c * P + 128],
                                                        ACT.Copy, scale=yr[:, (s8 + 1) % 4, c, 1 + y:2 + y])
                    last.then_inc(e_ok, 1)

            act.wait_ge(ld_mp, 16 * 15)
            message_steps(act, radial)
            act.wait_ge(ld_mq, 16 * 8)
            scale_f = (2 * HID) ** -0.5
            for n in range(-2, BLOCKS):
                if n + 2 < BLOCKS:
                    m = n + 2
                    r = rows(m)
                    act.wait_ge(q_t, m + 1)
                    after(act, q_o, m - 1)
                    nc.scalar.activation(agg_t[:, m % 2, 0:2, 0:r],
                                         ps[m % 2][:, 0:2 * P].rearrange("p (j n) -> p j n", j=2)[:, :, 0:r], ACT.Copy)
                    nc.scalar.activation(agg_t[0:2 * HID, m % 2, 2, 0:r], ps[m % 2][0:2 * HID, 2 * P:2 * P + r], ACT.Copy)\
                        .then_inc(q_ev, 1)
                if 0 <= n + 1 < BLOCKS:
                    m = n + 1
                    r = rows(m)
                    bank = ps[2 + m % 2]
                    act.wait_ge(q_o, m + 1)
                    after(act, q_pe, m - 1)
                    nc.scalar.activation(ssp[:, m % 2, 0, 0:r], bank[:, 0:r], ACT.Abs, scale=scale_f).then_inc(act_o, 1)
                    nc.scalar.activation(ssp[:, m % 2, 2, 0:r], bank[:, 0:r], ACT.Relu, scale=scale_f)
                    for c in range(3):
                        nc.scalar.activation(sv_t[:, m % 2, c + 1, 0:r],
                                             (bank if c % 2 == 0 else ps[6 + m % 2])[:, (c + 1) * P:(c + 1) * P + r],
                                             ACT.Copy, scale=scale_f)
                    act.wait_ge(act_o, 2 * STEPS + 2 * m + 1)
                    nc.scalar.activation(ssp[:, m % 2, 1, 0:r], ssp[:, m % 2, 0, 0:r], ACT.Exp, scale=-1.0).then_inc(act_o, 1)
                    act.wait_ge(act_o, 2 * STEPS + 2 * m + 2)
                    nc.scalar.activation(ssp[:, m % 2, 0, 0:r], ssp[:, m % 2, 1, 0:r], ACT.Ln, bias=1.0).then_inc(q_act, 1)
            layernorm(3, xs, hs)
            for lay in range(2):
                for n in range(BLOCKS):
                    evacuate_transposed(rows(n), n)
                evacuate_aggregated()
                if lay == 0:
                    for n in range(BLOCKS):
                        r = rows(n)
                        act.wait_ge(lin_ok, 2 * BLOCKS + 2 * (n + 1))
                        nc.scalar.activation(hs[0:r, n, :], low[0:r, n % 2, :], ACT.Tanh).then_inc(act_h, n_h.up())

        @block.gpsimd
        def _(pool):
            nc.gpsimd.iota(pid_i[:, 0:1], pattern=[[0, 1]], base=0, channel_multiplier=1)
            nc.gpsimd.iota(pid[:, :], pattern=[[0, 1]], base=0, channel_multiplier=1,
                           allow_small_or_imprecise_dtypes=True)
            nc.gpsimd.iota(col_id[:, :], pattern=[[1, P]], base=0, channel_multiplier=0,
                           allow_small_or_imprecise_dtypes=True)
            nc.gpsimd.iota(iota_a[:, :], pattern=[[1, AWIN]], base=0, channel_multiplier=0,
                           allow_small_or_imprecise_dtypes=True)
            nc.gpsimd.iota(iota_w[:, :], pattern=[[1, WIN]], base=0, channel_multiplier=0,
                           allow_small_or_imprecise_dtypes=True)
            nc.gpsimd.memset(ones[:, :], 1.0)
            nc.gpsimd.memset(ones_b[:, :], 1.0)
            nc.gpsimd.memset(epsb[:, :], EPS)
            nc.gpsimd.memset(slot_i[:, :], 0)
            nc.gpsimd.memset(wc_blk[:, :], 0.0).then_inc(const, 1)
            nc.gpsimd.memset(zk[0], 0.0).then_inc(z_zero, 1)
            nc.gpsimd.memset(zk[1], 0.0).then_inc(z_zero, 1)
            pool.wait_ge(st_h, 16 * BLOCKS)
            pool.wait_ge(fit_ok, 1)
            pool.wait_ge(coef_ok, SLICES)

            def gather_ring(i, par, skip):
                for c in range(RING):
                    if c % QUAD == 0:
                        nc.gpsimd.tensor_copy(idx[:, 2 * par + c // QUAD, :],
                                              src_i[:, bass.ds(i * 2 * RING + par * RING + c, QUAD)]).then_inc(idx_ok, 1)
                    indexed = in_reg(pool, i * 4 + 2 * par + c // QUAD + 1)
                    used = in_reg(pool, i * 2 * RING + par * RING + c - RING + 1)
                    pool.wait_ge(fit_ok, 1)
                    if not skip:
                        pool.wait_ge(z_pe, used)
                    pool.wait_ge(idx_ok, indexed)
                    nc.gpsimd.indirect_dma_start(
                        out=gath[:, c, :], out_offset=None, in_=h_rows,
                        in_offset=bass.IndirectOffsetOnAxis(ap=idx[:, 2 * par + c // QUAD, c % QUAD:c % QUAD + 1], axis=0))\
                        .then_inc(gathered[c], 16)

            with pool.If(pool.value_load(fits[0:1, 0:1], min_val=0, max_val=1) == 1):
                for par in range(2):
                    gather_ring(0, par, par == 0)
                with pool.Fori(1, CHUNKS // RING // 2) as i:
                    for par in range(2):
                        gather_ring(i, par, False)
            with pool.Else():
                with pool.Fori(0, REAL_CHUNKS) as c:
                    used = in_reg(pool, c * WINDOWS + 1)
                    pool.wait_ge(fit_ok, 1)
                    pool.wait_ge(g_add, used)
                    nc.gpsimd.tensor_copy(idx[:, 0, 0:1], src_i[:, bass.ds(c, 1)]).then_inc(g_idx, 1)
                    indexed = in_reg(pool, c + 1)
                    pool.wait_ge(fit_ok, 1)
                    pool.wait_ge(g_idx, indexed)
                    nc.gpsimd.indirect_dma_start(
                        out=gath[:, 0, :], out_offset=None, in_=h_rows,
                        in_offset=bass.IndirectOffsetOnAxis(ap=idx[:, 0, 0:1], axis=0)).then_inc(g_gath, 16)
            pool.wait_ge(edges_done, 1)
            nc.gpsimd.memset(cnt[:, :, :].rearrange("p s d -> p (s d)").bitcast(i32), 0).then_inc(cnt_zero, 1)

            pool.wait_ge(rank_ok, 1)
            pool.wait_ge(st_zero, 32)

            def scatter_quad(g, par, lap, tail):
                at_i = att[:, par, :, :].bitcast(i32)
                loaded, copied = in_reg(pool, lap * 16 + 16), in_reg(pool, g + 1)
                pool.wait_ge(rank_ok, 1)
                pool.wait_ge(ld_att[par], loaded)
                nc.gpsimd.tensor_copy(at_i[:, :, DSTC:DSTC + 1], dst_i[:, bass.ds(g * QUAD, QUAD)].unsqueeze(2))
                nc.gpsimd.tensor_copy(att[:, par, :, SRCC:SRCC + 1], srclo[:, bass.ds(g * QUAD, QUAD)].unsqueeze(2))
                nc.gpsimd.tensor_copy(idx_s[:, par, :], slot_i[:, bass.ds(g * QUAD, QUAD)]).then_inc(att_ok, 1)
                pool.wait_ge(st_zero, 32)
                pool.wait_ge(att_ok, copied)
                for c in range(1 if tail else QUAD):
                    r = TAIL if tail else P
                    nc.gpsimd.indirect_dma_start(
                        out=slots, out_offset=bass.IndirectOffsetOnAxis(ap=idx_s[0:r, par, c:c + 1], axis=0),
                        in_=att[0:r, par, c, :], in_offset=None).then_inc(st_att[par], 16)

            def scatter_pair(i):
                for par in range(2):
                    scatter_quad(2 * i + par, par, i, False)

            with pool.Fori(0, REAL_QUADS // 2) as i:
                scatter_pair(i)
            scatter_quad(REAL_QUADS - 1, (REAL_QUADS - 1) % 2, REAL_QUADS // 2, True)
            pool.wait_ge(adj_ok, 1)
            for par in range(2):
                pool.wait_ge(st_att[par], ATT_DONE[par])
            nc.gpsimd.iota(iota_h[:, :], pattern=[[1, P]], base=0, channel_multiplier=0,
                           allow_small_or_imprecise_dtypes=True)
            nc.gpsimd.memset(w1_blk[:, :], 0.0)
            nc.gpsimd.memset(w2_blk[:, :], 0.0).then_inc(cnt_zero, 1)
            pool.wait_ge(st_u, 16 * BLOCKS)

            def gather_dst(st, par, s8):
                if not valid(st):
                    return
                loaded, used = in_reg(pool, lap16(st, s8)), in_reg(pool, st - QUAD + 1)
                pool.wait_ge(st_u, 16 * BLOCKS)
                pool.wait_ge(ld_at[s8 // QUAD], loaded)
                after(pool, m_ok, used)
                at_i = at[:, s8 // QUAD, s8 % QUAD, :, :].rearrange("p g (c w) -> p (g c) w", c=2).bitcast(i32)
                for c in range(QUAD):
                    nc.gpsimd.indirect_dma_start(
                        out=u[:, s8 % QUAD, c, :], out_offset=None, in_=u_rows,
                        in_offset=bass.IndirectOffsetOnAxis(ap=at_i[:, c, DSTC:DSTC + 1], axis=0))\
                        .then_inc(u_in[s8 % QUAD], 16)

            for st in range(8):
                gather_dst(st, st % 2, st % 8)
            with pool.Fori(1, STEPS // 8) as i:
                for s8 in range(8):
                    gather_dst(i * 8 + s8, s8 % 2, s8)
            for st in range(STEPS // 8 * 8, STEPS):
                gather_dst(st, st % 2, st % 8)

        @block.tensor
        def _(pe):
            mm = nc.tensor.matmul
            pe.wait_ge(const, 2)
            pe.wait_ge(win_out, 1)
            mm(ps[5][:, 0:CHUNKS], ones[0:1, :], win_f[0:1, :], start=True, stop=True).then_inc(win_pe, 1)
            pe.wait_ge(cnt_in, 1)
            mm(ps[6][0:1, 0:1], inside[:, 0:1], ones[:, 0:1], start=True, stop=True).then_inc(cnt_pe, 1)
            pe.wait_ge(ld_wc, 16 * QUAD)
            for j in range(CHUNKS // QUAD // ETS):
                pe.wait_ge(et_hot, j + 1)
                if j >= 5:
                    pe.wait_ge(coef_ok, j - 4)
                for g in range(ETS):
                    last = mm(ps[j % 5][:, g * QUAD * BASES:(g + 1) * QUAD * BASES], et_1[:, j % 2, g * P:(g + 1) * P],
                              wc_blk[:, :], start=True, stop=True)
                last.then_inc(coef_pe, 1)
            pe.wait_ge(fit_ok, 1)
            pe.wait_ge(coef_ok, SLICES)
            fit = pe.value_load(fits[0:1, 0:1], min_val=0, max_val=1)

            def add_edges(bank, h_slot, s_of):
                for k in range(KIN):
                    last = mm(bank[:, k * P:(k + 1) * P], gath[:, h_slot, k * P:(k + 1) * P],
                              s_of.rearrange("p b d -> p (b d)"), start=True, stop=True)
                return last

            def edge_pair(i, first):
                for par in range(2):
                    pe.wait_ge(spread_ok, i * 2 + par + 1)
                    for q in range(QUAD):
                        slot = par * QUAD + q
                        pe.wait_ge(gathered[slot], i * 16 + 16)
                        if not first:
                            pe.wait_ge(z_add, i * RING + slot - RING + 2)
                        add_edges(ps[slot], slot, spread[:, par, q, :, :]).then_inc(z_pe, 1)

            with pe.If(fit == 1):
                edge_pair(0, True)
                with pe.Fori(1, CHUNKS // RING) as i:
                    edge_pair(i, False)
            with pe.Else():
                with pe.Fori(0, REAL_CHUNKS) as c:
                    with pe.Fori(0, WINDOWS) as k:
                        pe.wait_ge(g_gath, c * 16 + 16)
                        pe.wait_ge(g_spread, c * WINDOWS + k + 1)
                        add_edges(ps[0], 0, spread[:, 0, 0, :, :]).then_inc(g_pe, 1)

            for k in range(BLOCKS):
                pe.wait_ge(in_ok, k + 1)
                mm(ps[5][:, 0:CHUNKS], below[:, :], in_blk, start=True, stop=True)
                mm(ps[6][:, 0:CHUNKS], ones_b[:, :], in_blk, start=True, stop=True).then_inc(rank_pe, 1)
            pe.wait_ge(edges_done, 1)

            def base_products(with_counts):
                for half in range(2):
                    for b in range(BASES):
                        for k in range(KIN):
                            use = half * BASES + b
                            pe.wait_ge(ld_base[k], 16 * (use + 1))
                            for j in range(BLOCKS // 2):
                                n = half * (BLOCKS // 2) + j
                                if half and b == 0 and k == 0:
                                    pe.wait_ge(o_free, j + 1)
                                last = mm(ps[j][0:rows(n), :], z[:, k, b, n * P:n * P + rows(n)], base_t[:, k, :],
                                          start=(b == 0 and k == 0), stop=(b == BASES - 1 and k == KIN - 1))
                                if j == BLOCKS // 2 - 1:
                                    last.then_inc(tile_pe, 1)
                                if with_counts:
                                    t = (use * KIN + k) * (BLOCKS // 2) + j
                                    pe.wait_ge(hot_ok, t + 1)
                                    if t >= 2:
                                        pe.wait_ge(a_add, t)
                                    mm(ps[5 + t % 2][:, 0:AWIN], hot_s[:, t % 2, :], hot_d[:, t % 2, :],
                                       start=True, stop=True).then_inc(a_pe, 1)
                    mm(ps[7][0:1, 0:1], ones[:, 0:1], ones[:, 0:1], start=True, stop=True).then_inc(half_pe, 1)

            with pe.If(fit == 1):
                base_products(True)
            with pe.Else():
                with pe.Fori(0, REAL_CHUNKS) as c:
                    with pe.Fori(0, WINDOWS) as k:
                        pe.wait_ge(ga_hot, c * WINDOWS + k + 1)
                        mm(ps[5][:, 0:AWIN], hot_s[:, 0, :], hot_d[:, 0, :], start=True, stop=True).then_inc(ga_pe, 1)
                base_products(False)

            pe.wait_ge(adj_ok, 1)
            for n in range(BLOCKS):
                r = rows(n)
                for s in range(BLOCKS):
                    last = mm(ps[7][0:r, n:n + 1], adj[0:rows(s), s, n * P:n * P + r], ones[0:rows(s), 0:1],
                              start=(s == 0), stop=(s == BLOCKS - 1))
            last.then_inc(deg_pe, 1)

            n_agg, n_lin = Count(), Count()
            ready = Count()

            def transpose_block(n):
                r = rows(n)
                after(pe, gt_ok, n_agg.n - 3)
                bank = ps[n_agg.n % 4]
                n_agg.up()
                for k in range(KIN):
                    last = nc.tensor.transpose(bank[:, k * P:k * P + r], hs[0:r, n, k * P:(k + 1) * P], ident[0:r, 0:r])
                last.then_inc(agg_pe, 1)

            def aggregate(h_sem, h_base):
                for j, (a, b) in enumerate(COLS):
                    for k in range(KIN):
                        after(pe, gt_ok, n_agg.n - 3)
                        bank = ps[n_agg.n % 4]
                        n_agg.up()
                        for s in range(BLOCKS):
                            if j == 0 and k == 0:
                                pe.wait_ge(h_sem, h_base + s + 1)
                            last = mm(bank[:, 0:b - a], hs[0:rows(s), s, k * P:(k + 1) * P], adj[0:rows(s), s, a:b],
                                      start=(s == 0), stop=(s == BLOCKS - 1))
                        last.then_inc(agg_pe, 1)

            def product(n, t, w):
                r = rows(n)
                after(pe, lin_ok, n_lin.n - 3)
                bank = ps[4 + n_lin.n % 4]
                n_lin.up()
                for k in range(KIN):
                    last = mm(bank[0:r, :], t[:, k, n * P:n * P + r], w[:, k, :], start=(k == 0), stop=(k == KIN - 1))
                last.then_inc(lin_pe, 1)

            def aggregated(n):
                end = n * P + rows(n)
                part_of = next(j for j, (a, b) in enumerate(COLS) if end <= b)
                pe.wait_ge(gt_ok, n_agg.n - (len(COLS) - 1 - part_of) * KIN)

            for conv in range(2):
                aggregate(ln_h if conv == 0 else act_h, BLOCKS if conv == 0 else 0)
                pe.wait_ge(ld_w12, 64)
                for n in range(BLOCKS):
                    aggregated(n)
                    product(n, gt, wa if conv == 0 else wb)

            pe.wait_ge(ld_mp, 16 * 15)
            for n in range(BLOCKS + 1):
                if n < BLOCKS:
                    pe.wait_ge(ln_h, 2 * BLOCKS + n + 1)
                    r = rows(n)
                    after(pe, gt_ok, n_agg.n - 3)
                    bank = ps[n_agg.n % 4]
                    n_agg.up()
                    nc.tensor.transpose(bank[:, 0:r], hs[0:r, n, 0:P], ident[0:r, 0:r])
                    for c in range(3):
                        last = nc.tensor.transpose(bank[:, (c + 1) * P:(c + 1) * P + r], hs[0:r, n, P + c:FEAT:3],
                                                   ident[0:r, 0:r])
                    last.then_inc(agg_pe, 1)
                if n:
                    m, r = n - 1, rows(n - 1)
                    pe.wait_ge(gt_ok, n_agg.n - (1 if n < BLOCKS else 0))
                    if m < 2:
                        pe.wait_ge(lin_ok, 2 * BLOCKS)
                    after(pe, u_ev, m - 1)
                    for j in range(4):
                        last = mm(ps[4 + m % 2][0:r, j * HID:(j + 1) * HID], ht[:, j, m * P:m * P + r],
                                  (ws_t if j == 0 else wv_t)[:, :], start=True, stop=True)
                    last.then_inc(u_pe, 1)
            pe.wait_ge(pre_ok, 2)

            def message(st, par, s8):
                if valid(st + 3):
                    sl = (s8 + 3) % 8
                    pe.wait_ge(ld_at[sl // QUAD], lap16(st + 3, s8 + 3))
                    after(pe, t_act, st + 3)
                    if isinstance(st, int) and st == -3:
                        pe.wait_ge(u_ev, BLOCKS)
                    nc.tensor.transpose(ps[2][:, 0:P], at[:, sl // QUAD, sl % QUAD, :, :].rearrange("p g w -> p (g w)"),
                                        ident[:, :]).then_inc(t_pe, 1)
                if valid(st + 2):
                    pe.wait_ge(t_act, st + 3)
                    after(pe, h_act, 2 * (st + 2))
                    mm(ps[3][:, 0:P], w1_blk[:, :], at_t[:, par, :], start=True, stop=True).then_inc(h_pe, 1)
                if valid(st + 1):
                    pe.wait_ge(h_ok, st + 2)
                    after(pe, e_ok, st)
                    after(pe, p_ok, st)
                    mm(ps[1 - par][:, :], ones_b[0:1, :], b2_r[0:1, 0:1, :].broadcast_to([1, QUAD, P]), start=True, stop=False)
                    mm(ps[1 - par][:, :], ones_b[0:1, :], b2_r[0:1, 1:2, :].broadcast_to([1, QUAD, P]), start=False, stop=False)
                    mm(ps[1 - par][:, :], ones_b[0:1, :], b2_r[0:1, 2:3, :].broadcast_to([1, QUAD, P]), start=False, stop=False)
                    mm(ps[1 - par][:, :], hid[:, 1 - par, :], w2_blk[:, :], start=False, stop=True).then_inc(w_pe, 1)
                if valid(st):
                    pe.wait_ge(m_ok, st + 1)
                    for g in range(2):
                        after(pe, m_add, 2 * st + g - 3)
                        for c in range(2):
                            last = mm(ps[4 + 2 * par + g][:, 0:MSG], hot[:, par, 2 * g + c, :], msg[:, par, 2 * g + c, :],
                                      start=(c == 0), stop=(c == 1))
                        last.then_inc(m_pe, 1)

            message_steps(pe, message)
            pe.wait_ge(ld_mq, 16 * 8)
            pe.wait_ge(m_add, GROUPS)
            pe.wait_ge(q_x, 1)
            for n in range(-2, BLOCKS):
                if n + 2 < BLOCKS:
                    m = n + 2
                    r = rows(m)
                    after(pe, q_ev, m - 1)
                    for j, (a, b) in enumerate(((0, 128), (128, 256), (256, 320))):
                        last = nc.tensor.transpose(ps[m % 2][0:b - a, j * P:j * P + r], agg[0:r, m * MSG + a:m * MSG + b],
                                                   ident[0:r, 0:r])
                    last.then_inc(q_t, 1)
                if 0 <= n + 1 < BLOCKS:
                    m = n + 1
                    r = rows(m)
                    bank = ps[2 + m % 2]
                    pe.wait_ge(q_ev, m + 1)
                    after(pe, q_act, m - 1)
                    mm(bank[:, 0:r], os_t, agg_t[:, m % 2, 0, 0:r], start=True, stop=True)
                    for c in range(3):
                        h = slice(2 * HID * (c % 2), 2 * HID * (c % 2 + 1))
                        to = bank if c % 2 == 0 else ps[6 + m % 2]
                        last = mm(to[:, (c + 1) * P:(c + 1) * P + r], ov_t[h, :], agg_t[h, m % 2, 1 + c // 2, 0:r],
                                  start=True, stop=True)
                    last.then_inc(q_o, 1)
                if n >= 0:
                    r = rows(n)
                    bank = ps[4 + n % 2]
                    pe.wait_ge(q_ok, n + 1)
                    after(pe, q_x, n)
                    mm(bank[0:r, 0:P], sv_t[:, n % 2, 0, 0:r], qs_t, start=True, stop=True)
                    for c in range(3):
                        last = mm(bank[0:r, (c + 1) * P:(c + 2) * P], sv_t[:, n % 2, c + 1, 0:r], qv_t,
                                  start=True, stop=True)
                    last.then_inc(q_pe, 1)
            for lay in range(2):
                for n in range(BLOCKS):
                    if lay == 0:
                        pe.wait_ge(ln_h, 3 * BLOCKS + n + 1)
                        if n == 0:
                            pe.wait_ge(q_act, BLOCKS)
                            pe.wait_ge(q_x, BLOCKS + 1)
                    else:
                        pe.wait_ge(act_h, BLOCKS + n + 1)
                    transpose_block(n)
                pe.wait_ge(adj_ok, 2)
                aggregate(ln_h if lay == 0 else act_h, 3 * BLOCKS if lay == 0 else BLOCKS)
                pe.wait_ge(ld_w3 if lay == 0 else ld_w4, 64 if lay == 0 else 32)
                for n in range(BLOCKS):
                    aggregated(n)
                    product(n, gt, wa)
                    product(n, ht, wb)

        @block.vector
        def _(dve):
            v = nc.vector
            n_v = Count()

            def layernorm(k, src_t, ready, scaled=False):
                at_stat, at_std = {}, {}
                for i in range(BLOCKS + 3):
                    if i < BLOCKS:
                        ready(i)
                        v.bn_stats(stat6[0:rows(i), i, :], src_t[0:rows(i), i, :]).then_inc(dve_o, n_v.up())
                        at_stat[i] = n_v.n
                    if 1 <= i < BLOCKS + 1:
                        n, r = i - 1, rows(i - 1)
                        dve.wait_ge(dve_o, at_stat[n])
                        v.bn_aggr(mv[0:r, n, :], stat6[0:r, n, :]).then_inc(ln_stat, 1)
                    if 2 <= i < BLOCKS + 2:
                        n, r = i - 2, rows(i - 2)
                        dve.wait_ge(ln_std, BLOCKS * k + n + 1)
                        v.reciprocal(rstd[0:r, n:n + 1], std[0:r, n:n + 1]).then_inc(dve_o, n_v.up())
                        if scaled:
                            dve.wait_ge(dve_o, n_v.n)
                            v.tensor_tensor(rstd[0:r, n:n + 1], rstd[0:r, n:n + 1], dis[0:r, n:n + 1], ALU.mult)\
                                .then_inc(dve_o, n_v.up())
                        at_std[n] = n_v.n
                    if i >= 3:
                        n, r = i - 3, rows(i - 3)
                        dve.wait_ge(dve_o, at_std[n])
                        v.tensor_scalar(nmr[0:r, n:n + 1], mv[0:r, n, 0:1], rstd[0:r, n:n + 1], -1.0,
                                        ALU.mult, ALU.mult).then_inc(ln_rs, 1)

            dve.wait_ge(const, 1)
            v.tensor_scalar(ident[:, :], col_id[:, :], pid[:, :], None, ALU.is_equal)
            v.tensor_scalar(below[:, :], col_id[:, :], pid[:, :], None, ALU.is_gt).then_inc(const, 1)
            v.tensor_scalar(pid_i[:, 1:2], pid_i[:, 0:1], RELS - 1, None, ALU.bitwise_and).then_inc(dve_o, n_v.up())
            dve.wait_ge(dve_o, n_v.n)
            v.tensor_copy(rel_id[:, :], pid_i[:, 1:2]).then_inc(dve_o, n_v.up())
            dve.wait_ge(dve_o, n_v.n)
            dve.wait_ge(ld_tab, 48)
            v.tensor_scalar(win_f[0:1, :], dst_i[0:1, :], 0.0, float(DSTP - WIN), ALU.max, ALU.min).then_inc(win_out, 1)
            v.tensor_scalar(win_i[0:1, :], dst_i[0:1, :], 0.0, float(DSTP - WIN), ALU.max, ALU.min)
            v.tensor_scalar(tmp_i[:, :], src_i[:, :], P - 1, None, ALU.bitwise_and).then_inc(dve_o, n_v.up())
            dve.wait_ge(dve_o, n_v.n)
            v.tensor_copy(srclo[:, :], tmp_i[:, :])
            layernorm(0, x_in, lambda n: dve.wait_ge(ld_x[0 if n < 4 else 1 if n < 9 else 2], 16))
            v.tensor_scalar(tmp_i[:, :], src_i[:, :], 7, None, ALU.logical_shift_right).then_inc(dve_o, n_v.up())
            dve.wait_ge(win_pe, 1)
            v.tensor_tensor(tmp_a[:, :], dst_i[:, :], ps[5][:, 0:CHUNKS], ALU.subtract).then_inc(dve_o, n_v.up())
            dve.wait_ge(dve_o, n_v.n)
            v.tensor_scalar(offs[:, :], tmp_a[:, :], -1.0, float(WIN), ALU.max, ALU.min)
            v.tensor_scalar(tmp_b[:, :], tmp_a[:, :], 0.0, None, ALU.is_ge).then_inc(dve_o, n_v.up())
            dve.wait_ge(dve_o, n_v.n)
            v.scalar_tensor_tensor(tmp_b[:, :], tmp_a[:, :], WIN - 0.5, tmp_b[:, :], ALU.is_lt, ALU.mult)\
                .then_inc(dve_o, n_v.up())
            dve.wait_ge(dve_o, n_v.n)
            v.tensor_reduce(inside[:, :], tmp_b[:, :], mybir.AxisListType.X, ALU.add).then_inc(cnt_in, 1)
            v.scalar_tensor_tensor(tmp_a[:, :], tmp_a[:, :], float(BLOCKS), tmp_i[:, :], ALU.mult, ALU.add)\
                .then_inc(dve_o, n_v.up())
            dve.wait_ge(dve_o, n_v.n)
            v.tensor_scalar(acol[:, :], tmp_a[:, :], -1.0, float(AWIN), ALU.max, ALU.min)
            dve.wait_ge(cnt_pe, 1)
            v.tensor_scalar(fits[0:1, 0:1], ps[6][0:1, 0:1], EDGES - 0.5, None, ALU.is_ge).then_inc(fit_ok, 1)
            for j in range(SLICES + 1):
                if j < SLICES:
                    dve.wait_ge(ld_et[j % 2], 16 * QUAD * (j // 2 + 1))
                    if j >= 2:
                        dve.wait_ge(coef_pe, j - 1)
                    v.tensor_scalar(et_1[:, j % 2, :], et_i[:, j % 2, :], rel_id[:, :], None, ALU.is_equal)\
                        .then_inc(et_hot, 1)
                if j:
                    c = slice((j - 1) * ETS * QUAD, j * ETS * QUAD)
                    dve.wait_ge(coef_pe, j)
                    v.tensor_tensor(coef[:, c, :],
                                    ps[(j - 1) % 5][:, 0:ETS * QUAD * BASES].rearrange("p (t b) -> p t b", b=BASES),
                                    norm_f[:, c].unsqueeze(2).broadcast_to([P, ETS * QUAD, BASES]), ALU.mult)\
                        .then_inc(coef_ok, 1)

            def load4(ap, most):
                return nc.values_load_multi_w_load_instructions(
                    ap, engines=[mybir.EngineType.DVE], min_val=0, max_val=most,
                    skip_runtime_bounds_check_because="clamped or counted on the chip")[1]

            def make_hit(g, par):
                v.tensor_tensor(hit[:, par, :, :], iota_w[:, :].unsqueeze(1).broadcast_to([P, QUAD, WIN]),
                                offs[:, bass.ds(g * QUAD, QUAD)].unsqueeze(2).broadcast_to([P, QUAD, WIN]),
                                ALU.is_equal).then_inc(hit_ok, 1)

            def make_spread(g, par):
                dve.wait_ge(hit_ok, g + 1)
                v.tensor_tensor(spread[:, par, :, :, :],
                                hit[:, par, :, :].unsqueeze(2).broadcast_to([P, QUAD, BASES, WIN]),
                                coef[:, bass.ds(g * QUAD, QUAD), :].unsqueeze(3).broadcast_to([P, QUAD, BASES, WIN]),
                                ALU.mult).then_inc(spread_ok, 1)

            def add_chunk(t, bank, w):
                dve.wait_ge(z_pe, t + 1)
                dve.wait_ge(z_add, t + 1)
                zw = z[:, :, :, bass.ds(w, WIN)]
                v.tensor_tensor(zw, zw, bank[:, :].rearrange("p (k b d) -> p k b d", k=KIN, b=BASES), ALU.add)\
                    .then_inc(z_add, 1)

            def add_quad(g, par, further):
                w = load4(win_i[0:1, bass.ds(g * QUAD, QUAD)], DSTP - WIN)
                add_chunk(g * QUAD, ps[par * QUAD], w[0])
                if further:
                    make_hit(g + 2, par)
                add_chunk(g * QUAD + 1, ps[par * QUAD + 1], w[1])
                add_chunk(g * QUAD + 2, ps[par * QUAD + 2], w[2])
                if further:
                    dve.wait_ge(z_pe, g * QUAD + QUAD)
                    make_spread(g + 2, par)
                add_chunk(g * QUAD + 3, ps[par * QUAD + 3], w[3])

            dve.wait_ge(coef_ok, SLICES)
            for par in range(2):
                make_hit(par, par)
            dve.wait_ge(z_zero, 2)
            dve.wait_ge(z_zero_a, 2)
            dve.wait_ge(st_zero, 32)
            dve.wait_ge(fit_ok, 1)
            fit = dve.value_load(fits[0:1, 0:1], min_val=0, max_val=1)
            with dve.If(fit == 1):
                v.memset(turn[:, 0:1], 0.0).then_inc(z_add, 1)
                for par in range(2):
                    make_spread(par, par)
                with dve.Fori(0, CHUNKS // RING - 1) as i:
                    for par in range(2):
                        add_quad(i * 2 + par, par, True)
                for par in range(2):
                    add_quad(CHUNKS // QUAD - 2 + par, par, False)
                dve.wait_ge(z_add, CHUNKS + 1)
            with dve.Else():
                v.memset(turn[:, 0:1], 0.0).then_inc(g_add, 1)
                with dve.Fori(0, REAL_CHUNKS) as c:
                    v.tensor_scalar(one_off[:, 0:1], dst_i[:, bass.ds(c, 1)], 0.0, None, ALU.add).then_inc(g_o, 1)
                    with dve.Fori(0, WINDOWS) as k:
                        dve.wait_ge(g_o, c * (1 + 2 * WINDOWS) + k * 2 + 1)
                        v.tensor_scalar(hit[:, 0, 0, :], iota_w[:, :], one_off[:, 0:1], None, ALU.is_equal).then_inc(g_o, 1)
                        dve.wait_ge(g_o, c * (1 + 2 * WINDOWS) + k * 2 + 2)
                        v.tensor_scalar(one_off[:, 0:1], one_off[:, 0:1], -float(WIN), None, ALU.add).then_inc(g_o, 1)
                        v.tensor_tensor(spread[:, 0, 0, :, :],
                                        hit[:, 0, 0, :].unsqueeze(1).broadcast_to([P, BASES, WIN]),
                                        coef[:, bass.ds(c, 1), :].rearrange("p t b -> p (t b)").unsqueeze(2)
                                        .broadcast_to([P, BASES, WIN]), ALU.mult).then_inc(g_spread, 1)
                        dve.wait_ge(g_pe, c * WINDOWS + k + 1)
                        dve.wait_ge(g_add, c * WINDOWS + k + 1)
                        zw = z[:, :, :, bass.ds(k * WIN, WIN)]
                        v.tensor_tensor(zw, zw, ps[0][:, :].rearrange("p (k b d) -> p k b d", k=KIN, b=BASES), ALU.add)\
                            .then_inc(g_add, 1)
                dve.wait_ge(g_add, REAL_CHUNKS * WINDOWS + 1)
            v.memset(start_k[:, 0:1], 0.0).then_inc(edges_done, 1)

            v.tensor_scalar(blk_i, src_i[:, :], 7, None, ALU.logical_shift_right).then_inc(dve_o, n_v.up())
            dve.wait_ge(dve_o, n_v.n)
            v.tensor_copy(blk_f, blk_i).then_inc(dve_o, n_v.up())
            dve.wait_ge(dve_o, n_v.n)
            v.memset(blk_f[:, REAL_CHUNKS:CHUNKS], -1.0)
            v.memset(blk_f[TAIL:P, REAL_CHUNKS - 1:REAL_CHUNKS], -1.0)
            v.memset(slot_f, 0.0).then_inc(dve_o, n_v.up())
            for k in range(BLOCKS):
                dve.wait_ge(dve_o, n_v.n)
                v.tensor_scalar(in_blk, blk_f, float(k), None, ALU.is_equal).then_inc(in_ok, 1)
                dve.wait_ge(rank_pe, k + 1)
                v.tensor_tensor_scan(run_sum, ones[:, 0:1].to_broadcast([P, CHUNKS]), ps[6][:, 0:CHUNKS],
                                     start_k[:, k:k + 1], ALU.mult, ALU.add).then_inc(dve_o, n_v.up())
                dve.wait_ge(dve_o, n_v.n)
                v.tensor_scalar(sized_i[:, 0:1], run_sum[:, CHUNKS - 1:CHUNKS], GROUP - 1.0, None, ALU.add)\
                    .then_inc(dve_o, n_v.up())
                v.tensor_tensor(place, run_sum, ps[6][:, 0:CHUNKS], ALU.subtract).then_inc(dve_o, n_v.up())
                dve.wait_ge(dve_o, n_v.n - 1)
                v.tensor_scalar(sized_i[:, 1:2], sized_i[:, 0:1], 8, 8, ALU.logical_shift_right, ALU.logical_shift_left)\
                    .then_inc(dve_o, n_v.up())
                dve.wait_ge(dve_o, n_v.n - 1)
                v.tensor_tensor(place, place, ps[5][:, 0:CHUNKS], ALU.add).then_inc(dve_o, n_v.up())
                dve.wait_ge(dve_o, n_v.n - 1)
                v.tensor_copy(start_k[:, k + 1:k + 2], sized_i[:, 1:2]).then_inc(dve_o, n_v.up())
                dve.wait_ge(dve_o, n_v.n - 1)
                v.tensor_tensor(place, place, in_blk, ALU.mult).then_inc(dve_o, n_v.up())
                dve.wait_ge(dve_o, n_v.n)
                v.tensor_tensor(slot_f, slot_f, place, ALU.add).then_inc(dve_o, n_v.up())
            dve.wait_ge(dve_o, n_v.n)
            v.tensor_copy(slot_i[:, :], slot_f).then_inc(rank_ok, 1)

            def make_hot(t, par):
                v.tensor_scalar(hot_s[:, par, :], iota_a[:, 0:P], srclo[:, bass.ds(t, 1)], None, ALU.is_equal)
                v.tensor_scalar(hot_d[:, par, :], iota_a[:, :], acol[:, bass.ds(t, 1)], None, ALU.is_equal)\
                    .then_inc(hot_ok, 1)

            def count_quad(g, further):
                w = load4(win_i[0:1, bass.ds(g * QUAD, QUAD)], DSTP - WIN)
                for q in range(QUAD):
                    t = g * QUAD + q
                    dve.wait_ge(a_pe, t + 1)
                    if further or q < 2:
                        make_hot(t + 2, q % 2)
                    dve.wait_ge(a_add, t + 1)
                    cw = cnt[:, :, bass.ds(w[q], WIN)]
                    v.tensor_tensor(cw, cw, ps[5 + q % 2][:, 0:AWIN].rearrange("p (d s) -> p s d", s=BLOCKS), ALU.add)\
                        .then_inc(a_add, 1)

            def evacuate_half(half):
                dve.wait_ge(half_pe, half + 1)
                for j in range(BLOCKS // 2):
                    m = half * (BLOCKS // 2) + j
                    r = rows(m)
                    dve.wait_ge(ld_xt[m % 2], 16 * (m // 2 + 1))
                    v.tensor_tensor(xt[0:r, m % 2, :], ps[j][0:r, :], xt[0:r, m % 2, :], ALU.add).then_inc(o_free, 1)
                    dve.wait_ge(o_free, m + 1)
                    v.tensor_tensor(xt[0:r, m % 2, :], xt[0:r, m % 2, :], bias0[0:r, :], ALU.add).then_inc(o_done, 1)

            dve.wait_ge(cnt_zero, 1)
            dve.wait_ge(ld_bias, 16)
            with dve.If(fit == 1):
                v.memset(turn[:, 1:2], 0.0).then_inc(a_add, 1)
                for t in range(2):
                    make_hot(t, t)
                with dve.Fori(0, CHUNKS // QUAD // 2) as g:
                    count_quad(g, True)
                evacuate_half(0)
                with dve.Fori(CHUNKS // QUAD // 2, CHUNKS // QUAD - 1) as g:
                    count_quad(g, True)
                count_quad(CHUNKS // QUAD - 1, False)
                dve.wait_ge(a_add, CHUNKS + 1)
                evacuate_half(1)
            with dve.Else():
                v.memset(turn[:, 1:2], 0.0).then_inc(ga_add, 1)
                with dve.Fori(0, REAL_CHUNKS) as c:
                    v.tensor_scalar(hot_s[:, 0, :], iota_a[:, 0:P], srclo[:, bass.ds(c, 1)], None, ALU.is_equal)
                    v.tensor_scalar(sized_i[:, 0:1], src_i[:, bass.ds(c, 1)], 7, None, ALU.logical_shift_right)
                    v.tensor_scalar(one_off[:, 1:2], dst_i[:, bass.ds(c, 1)], float(BLOCKS), None, ALU.mult)\
                        .then_inc(ga_o, 1)
                    dve.wait_ge(ga_o, c * (2 + WINDOWS) + 1)
                    v.tensor_tensor(one_off[:, 0:1], one_off[:, 1:2], sized_i[:, 0:1], ALU.add).then_inc(ga_o, 1)
                    with dve.Fori(0, WINDOWS) as k:
                        dve.wait_ge(ga_o, c * (2 + WINDOWS) + k + 2)
                        v.tensor_scalar(hot_d[:, 0, :], iota_a[:, :], one_off[:, 0:1], None, ALU.is_equal)\
                            .then_inc(ga_hot, 1)
                        dve.wait_ge(ga_pe, c * WINDOWS + k + 1)
                        v.tensor_scalar(one_off[:, 0:1], one_off[:, 0:1], -float(AWIN), None, ALU.add).then_inc(ga_o, 1)
                        dve.wait_ge(ga_add, c * WINDOWS + k + 1)
                        cw = cnt[:, :, bass.ds(k * WIN, WIN)]
                        v.tensor_tensor(cw, cw, ps[5][:, 0:AWIN].rearrange("p (d s) -> p s d", s=BLOCKS), ALU.add)\
                            .then_inc(ga_add, 1)
                dve.wait_ge(ga_add, REAL_CHUNKS * WINDOWS + 1)
                for half in range(2):
                    evacuate_half(half)
            v.memset(deg[:, :], 1.0).then_inc(cnt_done, 1)

            for s in range(5):
                v.tensor_copy(adj[:, s, :], cnt[:, s, 0:NODES]).then_inc(dve_o, n_v.up())
            dve.wait_ge(dve_o, n_v.n)
            for n in range(BLOCKS):
                r = rows(n)
                if n >= 5:
                    dve.wait_ge(adj_act, n - 4)
                diag = adj[0:r, n, n * P:n * P + r]
                last = v.tensor_tensor(diag, diag, ident[0:r, 0:r], ALU.add)
            last.then_inc(adj_ok, 1)
            v.memset(seg_g[:, :], float(GROUP)).then_inc(dve_o, n_v.up())
            dve.wait_ge(dve_o, n_v.n)
            v.tensor_tensor_scan(seg_f[:, :], ones[0:1, 0:1].to_broadcast([1, GROUPS]), seg_g[:, :], -float(GROUP),
                                 ALU.mult, ALU.add).then_inc(dve_o, n_v.up())
            dve.wait_ge(dve_o, n_v.n)
            v.memset(seg_g[:, :], 0.0).then_inc(dve_o, n_v.up())
            for k in range(1, BLOCKS):
                dve.wait_ge(dve_o, n_v.n)
                v.scalar_tensor_tensor(seg_g[:, :], seg_f[:, :], start_k[0:1, k:k + 1], seg_g[:, :], ALU.is_ge, ALU.add)\
                    .then_inc(dve_o, n_v.up())
            dve.wait_ge(dve_o, n_v.n)
            v.tensor_scalar(seg_i[:, :], seg_g[:, :], float(MSG), None, ALU.mult).then_inc(dve_o, n_v.up())
            dve.wait_ge(deg_pe, 1)
            v.tensor_copy(deg[:, 0:BLOCKS - 1], ps[7][:, 0:BLOCKS - 1])
            v.tensor_copy(deg[0:LAST, BLOCKS - 1:BLOCKS], ps[7][0:LAST, BLOCKS - 1:BLOCKS]).then_inc(deg_ok, 1)
            dve.wait_ge(deg_ok, 1)
            v.tensor_scalar(inv[:, :], deg[:, :], -1.0, 1.0, ALU.add, ALU.max).then_inc(dve_o, n_v.up())
            dve.wait_ge(dve_o, n_v.n)
            v.reciprocal(inv[:, :], inv[:, :])
            dve.wait_ge(deg_sq, 1)
            v.reciprocal(dis[:, :], dis[:, :]).then_inc(dve_o, n_v.up())
            dve.wait_ge(dve_o, n_v.n)
            dve.wait_ge(ld_x1, 32)
            layernorm(1, xs, lambda n: None, scaled=True)

            def add_bias(k):
                for n in range(BLOCKS):
                    r = rows(n)
                    dve.wait_ge(ln_h, BLOCKS * k + n + 1)
                    v.tensor_tensor(xs[0:r, n, :], xs[0:r, n, :], b_b[0:r, :], ALU.add).then_inc(dve_o, n_v.up())
                dve.wait_ge(dve_o, n_v.n)

            def lin_bank(unit):
                dve.wait_ge(lin_pe, unit + 1)
                return ps[4 + unit % 4]

            dve.wait_ge(ld_w12, 64)
            add_bias(1)
            for n in range(BLOCKS):
                r = rows(n)
                bank = lin_bank(n)
                if n >= 2:
                    dve.wait_ge(act_h, n - 1)
                v.scalar_tensor_tensor(low[0:r, n % 2, :], bank[0:r, :], dis[0:r, n:n + 1], b_a[0:r, :], ALU.mult, ALU.add)\
                    .then_inc(lin_ok, 1)
            for n in range(BLOCKS):
                r = rows(n)
                bank = lin_bank(BLOCKS + n)
                v.scalar_tensor_tensor(xs[0:r, n, :], bank[0:r, :], dis[0:r, n:n + 1], xs[0:r, n, :], ALU.mult, ALU.add)\
                    .then_inc(lin_ok, 1)
            layernorm(2, xs, lambda n: dve.wait_ge(lin_ok, BLOCKS + n + 1))

            dve.wait_ge(ld_mp, 16 * 15)
            b2, left = b2_f[0:1, 0, :], b2_f[0:1, 1, :]
            v.tensor_copy(b2_r[0:1, 0, :], b2).then_inc(dve_o, n_v.up())
            dve.wait_ge(dve_o, n_v.n)
            v.tensor_tensor(left, b2, b2_r[0:1, 0, :], ALU.subtract).then_inc(dve_o, n_v.up())
            dve.wait_ge(dve_o, n_v.n)
            v.tensor_copy(b2_r[0:1, 1, :], left).then_inc(dve_o, n_v.up())
            dve.wait_ge(dve_o, n_v.n)
            v.tensor_tensor(b2_r[0:1, 2, :], left, b2_r[0:1, 1, :], ALU.subtract).then_inc(pre_ok, 1)
            v.memset(agg, 0.0).then_inc(pre_ok, 1)
            for n in range(BLOCKS):
                diag = adj[0:rows(n), n, n * P:n * P + rows(n)]
                last = v.tensor_tensor(diag, diag, ident[0:rows(n), 0:rows(n)], ALU.subtract)
            last.then_inc(adj_ok, 1)

            def slot_words(s8, a, b):
                s8 = s8 % 8
                return at[:, s8 // QUAD, s8 % QUAD, :, :].rearrange("p g (c w) -> p (g c) w", c=2)[:, :, a:b]

            def messages(st, par, s8):
                us = u[:, s8 % QUAD, :, 0:HID]
                uv = u[:, s8 % QUAD, :, HID:P].rearrange("p c (y f) -> p c y f", y=3)
                v_in = msg[:, par, :, P:MSG].rearrange("p c (y f) -> p c y f", y=3)
                after(dve, m_pe, 2 * st - 2)
                v.tensor_tensor(hot[:, par, :, :], iota_h[:, :].unsqueeze(1).broadcast_to([P, QUAD, P]),
                                slot_words(s8, SRCC, SRCC + 1).broadcast_to([P, QUAD, P]), ALU.is_equal)
                dve.wait_ge(p_ok, st + 1)
                dve.wait_ge(u_in[s8 % QUAD], 64 * (s8 // QUAD) + 64 + (st - s8) * 16)
                v.tensor_tensor(msg[:, par, :, 0:HID], py[:, par, :, 0:HID], us, ALU.mult)
                v.tensor_tensor(v_in[:, :, :, HID:2 * HID],
                                py[:, par, :, HID:2 * HID].unsqueeze(2).broadcast_to([P, QUAD, 3, HID]), uv, ALU.mult)
                v.tensor_tensor(msg[:, par, :, HID:P].rearrange("p c (y f) -> p c y f", y=3),
                                ey[:, par, :, :, 0:HID], uv, ALU.mult)
                v.tensor_tensor(v_in[:, :, :, 0:HID], ey[:, par, :, :, HID:2 * HID],
                                us.unsqueeze(2).broadcast_to([P, QUAD, 3, HID]), ALU.mult).then_inc(m_ok, 1)

            seg_at = {}

            def message(st, par, s8):
                if valid(st):
                    messages(st, par, s8)
                if valid(st + 2):
                    dve.wait_ge(h_act, 2 * (st + 3))
                    after(dve, w_pe, st + 1)
                    v.scalar_tensor_tensor(hid[:, par, :], soft[:, par, 0, :], -LOG2, soft[:, par, 2, :],
                                           ALU.add, ALU.add).then_inc(h_ok, 1)
                    after(dve, e_ok, st - 1)
                    dve.wait_ge(ld_at[(s8 + 2) % 8 // QUAD], lap16(st + 2, s8 + 2))
                    v.tensor_tensor(yr[:, (s8 + 2) % 4, :, :], slot_words(s8 + 2, YCOL, YCOL + 4),
                                    slot_words(s8 + 2, RCUT, RCUT + 1).broadcast_to([P, QUAD, 4]), ALU.mult)\
                        .then_inc(y_ok, 1)
                if valid(st + 1):
                    dve.wait_ge(e_ok, st + 2)
                    dve.wait_ge(y_ok, st + 2)
                    v.tensor_tensor(py[:, 1 - par, :, :],
                                    ps[1 - par][:, :].rearrange("p (c w) -> p c w", c=QUAD)[:, :, 0:2 * HID],
                                    yr[:, (s8 + 1) % 4, :, 0:1].broadcast_to([P, QUAD, 2 * HID]), ALU.mult)\
                        .then_inc(p_ok, 1)
                if s8 % 2 == 0 and valid(st):
                    if isinstance(st, int) and st == 0:
                        seg_at[0] = [None, None] + list(load4(seg_i[0:1, 0:QUAD], MSG * (BLOCKS - 1))[0:2])
                    else:
                        seg_at[0] = load4(seg_i[0:1, bass.ds(st * 2 - 2, QUAD)], MSG * (BLOCKS - 1))
                if not (isinstance(st, int) and st < 1):
                    add_groups(st - 1, 1 - par, seg_at[0][0:2] if par == 0 else seg_at[0][2:4])

            def add_groups(st, par, seg):
                for g in range(2):
                    dve.wait_ge(m_pe, 2 * st + g + 1)
                    dve.wait_ge(m_add, 2 * st + g)
                    a = agg[:, bass.ds(seg[g], MSG)]
                    v.tensor_tensor(a, a, ps[4 + 2 * par + g][:, 0:MSG], ALU.add).then_inc(m_add, 1)

            message_steps(dve, message)
            add_groups(STEPS - 1, (STEPS - 1) % 2, load4(seg_i[0:1, GROUPS - QUAD:GROUPS], MSG * (BLOCKS - 1))[2:4])
            dve.wait_ge(ld_mq, 16 * 8)
            for a, b in ((HID, 2 * HID), (2 * HID, P)):
                last = v.tensor_scalar(os_t[a:b, :], os_t[a:b, :], IS3, None, ALU.mult)
            last.then_inc(q_x, 1)
            for n in range(-1, BLOCKS):
                if n + 1 < BLOCKS:
                    m, r = n + 1, rows(n + 1)
                    dve.wait_ge(q_act, m + 1)
                    after(dve, q_pe, m - 1)
                    v.scalar_tensor_tensor(sv_t[:, m % 2, 0, 0:r], ssp[:, m % 2, 0, 0:r], -LOG2, ssp[:, m % 2, 2, 0:r],
                                           ALU.add, ALU.add).then_inc(q_ok, 1)
                if n >= 0:
                    r = rows(n)
                    bank = ps[4 + n % 2]
                    dve.wait_ge(q_pe, n + 1)
                    v.scalar_tensor_tensor(xs[0:r, n, 0:P], bank[0:r, 0:P], P ** -0.5, xs[0:r, n, 0:P],
                                           ALU.mult, ALU.add)
                    xv = xs[0:r, n, P:FEAT].rearrange("p (d c) -> p c d", c=3)
                    v.scalar_tensor_tensor(xv, bank[0:r, P:FEAT].rearrange("p (c d) -> p c d", c=3), P ** -0.5, xv,
                                           ALU.mult, ALU.add).then_inc(q_x, 1)
            layernorm(3, xs, lambda n: dve.wait_ge(q_x, n + 2))
            dve.wait_ge(ld_w3, 64)
            add_bias(3)
            for lay in range(2):
                for n in range(BLOCKS):
                    r = rows(n)
                    unit = 2 * BLOCKS * (lay + 1) + 2 * n
                    bank = lin_bank(unit)
                    if lay == 0 and n >= 2:
                        dve.wait_ge(act_h, BLOCKS + n - 1)
                    if lay == 1:
                        dve.wait_ge(act_h, 2 * BLOCKS)
                        after(dve, st_o[n % 2], 16 * (n // 2))
                    v.scalar_tensor_tensor(low[0:r, n % 2, :], bank[0:r, :], inv[0:r, n:n + 1],
                                           b_a[0:r, :] if lay == 0 else xs[0:r, n, :], ALU.mult, ALU.add)\
                        .then_inc(lin_ok, 1)
                    bank = lin_bank(unit + 1)
                    dve.wait_ge(lin_ok, unit + 1)
                    v.tensor_tensor(low[0:r, n % 2, :], low[0:r, n % 2, :], bank[0:r, :], ALU.add).then_inc(lin_ok, 1)


def kernel(x, src, dst, edge_attr_20, edge_attr_4, edge_type_32, edge_weight, edge_weight1, L0_gnn_bases, L0_gnn_w_comp,
           L0_gnn_h_bias, L1_gnn_W1, L1_gnn_b1, L1_gnn_W2, L1_gnn_b2, L2_gnn_w_in2f_s, L2_gnn_w_in2f_v, L2_gnn_W1,
           L2_gnn_b1, L2_gnn_W2, L2_gnn_b2, L2_gnn_w_f2o1_s, L2_gnn_w_f2o1_v, L2_gnn_w_f2o2_s, L2_gnn_w_f2o2_v,
           L3_gnn_label, L3_gnn_W1_l, L3_gnn_W1_r, L3_gnn_b1, L3_gnn_W2_l, L3_gnn_W2_r, L3_gnn_b2):
    import numpy as np
    import concourse.bacc as bacc
    from concourse.bass_utils import run_bass_kernel_spmd

    def by_chunks(a, fill=0):
        a = np.asarray(a).reshape(EDGES, -1)
        pad = np.full((CHUNKS * P - EDGES, a.shape[1]), fill, a.dtype)
        return np.concatenate([a, pad]).reshape(CHUNKS, P, -1).transpose(1, 0, 2)

    order = [0, 3, 1, 2]
    f32 = np.float32
    etype = by_chunks(edge_type_32)[:, :, 0].reshape(P, CHUNKS // QUAD, QUAD).transpose(2, 1, 0).reshape(QUAD, -1)
    words = [np.asarray(edge_attr_20), np.asarray(edge_attr_4), np.asarray(edge_weight).reshape(EDGES, 1),
             np.zeros((EDGES, ROW - RCUT - 1), f32)]
    arrays = dict(
        src=by_chunks(src)[:, :, 0], dst=by_chunks(dst, PADDST)[:, :, 0], etype=etype,
        norm=by_chunks(edge_weight1)[:, :, 0], attr=by_chunks(np.concatenate(words, axis=1)), x=x,
        bases=L0_gnn_bases, w_comp=L0_gnn_w_comp, h_bias=np.asarray(L0_gnn_h_bias).reshape(1, FEAT),
        g_w1=L1_gnn_W1, g_b1=np.asarray(L1_gnn_b1).reshape(1, FEAT), g_w2=L1_gnn_W2,
        g_b2=np.asarray(L1_gnn_b2).reshape(1, FEAT),
        m_ws=L2_gnn_w_in2f_s, m_wv=L2_gnn_w_in2f_v, m_w1=L2_gnn_W1, m_b1=np.asarray(L2_gnn_b1).reshape(HID, 1),
        m_w2=np.asarray(L2_gnn_W2).reshape(HID, HID, 6)[:, :, order].transpose(0, 2, 1).reshape(HID, 4 * HID),
        m_b2=np.asarray(L2_gnn_b2).reshape(HID, 6)[:, order].T.reshape(1, 4 * HID),
        m_os=L2_gnn_w_f2o1_s, m_ov=L2_gnn_w_f2o1_v, m_qs=L2_gnn_w_f2o2_s, m_qv=L2_gnn_w_f2o2_v,
        s_w1l=np.asarray(L3_gnn_W1_l).T, s_w1r=np.asarray(L3_gnn_W1_r).T, s_b1=np.asarray(L3_gnn_b1).reshape(1, FEAT),
        s_w2l=np.asarray(L3_gnn_W2_l).T, s_w2r=np.asarray(L3_gnn_W2_r).T, s_b2=np.asarray(L3_gnn_b2).reshape(1, FEAT))

    nc = bacc.Bacc("TRN2", target_bir_lowering=False, num_devices=1)
    ins, args = {}, {}
    for name, a in arrays.items():
        a = np.ascontiguousarray(a)
        ins[f"in_{name}_dram"] = a
        args[name] = nc.dram_tensor(f"in_{name}_dram", a.shape, mybir.dt.from_np(a.dtype), kind="ExternalInput").ap()
    args["out"] = nc.dram_tensor("out_0_dram", (NODES, FEAT), mybir.dt.float32, kind="ExternalOutput").ap()
    graph_layers(nc, **args)
    r = run_bass_kernel_spmd(nc, [ins], core_ids=[0])
    return r.results[0]["out_0_dram"]
```

```python
import concourse.bass as bass
from concourse import mybir
from contextlib import ExitStack

P = 128
NODES, FEAT, EDGES = 1250, 512, 40000
BLOCKS = -(-NODES // P)
LAST = NODES - (BLOCKS - 1) * P
HALF = BLOCKS // 2
KIN = FEAT // P
CHUNKS = 320
REAL_CHUNKS = -(-EDGES // P)
TAIL = EDGES - (REAL_CHUNKS - 1) * P
BASES, RELS = 8, 32
WIN = 16
WINDOWS = -(-NODES // WIN)
DSTP = WINDOWS * WIN
AWIN = WIN * BLOCKS
FULL_QUADS = REAL_CHUNKS // 4
REST = REAL_CHUNKS - 4 * FULL_QUADS
RING = 8
QUAD = 4
GROUP = 2 * P
STEPS = 84
GROUPS = 2 * STEPS
RADIALS = STEPS // QUAD
SLOTS = GROUPS * GROUP
ROW = 32
ZROW = 256
FILLS = 6
YCOL, RCUT, DSTC, SRCC = 20, 24, 25, 26
RAD, HID = 20, 32
MSG = 256
PADDST = 4096
LOG2 = 0.6931471805599453
IS3 = 3.0 ** -0.5
EPS = 1e-5
COLS = [(0, 417), (417, 834), (834, 1250)]
ETS = 8
SLICES = CHUNKS // QUAD // ETS
assert EDGES // GROUP + BLOCKS <= GROUPS


def rows(n):
    return P if n < BLOCKS - 1 else LAST


class Count:

    def __init__(self):
        self.n = 0

    def up(self):
        self.n = self.n + 1
        return 1


def graph_layers(nc, src, dst, etype, norm, attr, x, bases, w_comp, h_bias, g_w1, g_b1, g_w2, g_b2,
                 m_ws, m_wv, m_w1, m_b1, m_w2, m_b2, m_os, m_ov, m_qs, m_qv,
                 s_w1l, s_w1r, s_b1, s_w2l, s_w2r, s_b2, out):
    f32, f16, bf16 = mybir.dt.float32, mybir.dt.float16, mybir.dt.bfloat16
    i32, u16 = mybir.dt.int32, mybir.dt.uint16
    ALU, ACT = mybir.AluOpType, mybir.ActivationFunctionType

    h_rows = nc.dram_tensor("h_rows", (NODES, FEAT), f32).ap()
    x1_rows = nc.dram_tensor("x1_rows", (HALF * P, FEAT), f32).ap()
    slots = nc.dram_tensor("slots", (SLOTS, ROW), f32).ap()
    u_rows = nc.dram_tensor("u_rows", (NODES, P), f32).ap()

    ctx = ExitStack()
    with ctx:
        def sb(scope, name, shape, dt):
            return scope.enter_context(nc.sbuf_tensor(name, shape, dt))

        def sem(name):
            return ctx.enter_context(nc.semaphore(name))

        ident = sb(ctx, "ident", [P, P], f32)
        ones = sb(ctx, "ones", [P, P], f32)
        below = sb(ctx, "below", [P, P], bf16)
        ones_b = sb(ctx, "ones_b", [P, P], bf16)
        iota_a = sb(ctx, "iota_a", [P, AWIN], f16)
        src_i = sb(ctx, "src_i", [P, CHUNKS], i32)
        dst_i = sb(ctx, "dst_i", [P, CHUNKS], i32)
        acol = sb(ctx, "acol", [P, CHUNKS], f16)
        srclo = sb(ctx, "srclo", [P, CHUNKS], f16)
        win_i = sb(ctx, "win_i", [1, CHUNKS], i32)
        slot_i = sb(ctx, "slot_i", [P, CHUNKS], i32)
        fits = sb(ctx, "fits", [1, 1], i32)
        start_k = sb(ctx, "start_k", [P, BLOCKS + 1], f32)
        idx_s = sb(ctx, "idx_s", [P, 2, QUAD], i32)
        stat6 = sb(ctx, "stat6", [P, BLOCKS, 6], f32)
        mv = sb(ctx, "mv", [P, BLOCKS, 2], f32)
        std = sb(ctx, "std", [P, BLOCKS], f32)
        rstd = sb(ctx, "rstd", [P, BLOCKS], f32)
        nmr = sb(ctx, "nmr", [P, BLOCKS], f32)
        epsb = sb(ctx, "epsb", [P, 1], f32)
        iota_w = sb(ctx, "iota_w", [P, WIN], f32)
        sized_i = sb(ctx, "sized_i", [P, 2], i32)
        one_off = sb(ctx, "one_off", [P, 2], f32)
        turn = sb(ctx, "turn", [P, 2], f32)

        z_scope = ExitStack()
        z = sb(z_scope, "z", [P, KIN, BASES, DSTP], f32)
        zk = [z[:, k, :, :].rearrange("p b d -> p (b d)") for k in range(KIN)]
        x_in = zk[KIN - 1][:, 0:BLOCKS * FEAT].rearrange("p (n f) -> p n f", f=FEAT)
        coef_scope = ExitStack()
        coef = sb(coef_scope, "coef", [P, CHUNKS, BASES], f32)
        offs = sb(coef_scope, "offs", [P, CHUNKS], f16)
        part = ExitStack()
        et_i = sb(part, "et_i", [P, 4, ETS * P], i32)
        et_1 = sb(part, "et_1", [P, 2, ETS * P], bf16)
        norm_f = sb(part, "norm_f", [P, CHUNKS], f32)
        wc_blk = sb(part, "wc_blk", [P, QUAD * BASES], f32)
        wc_part = sb(part, "wc_part", [P, 3, QUAD * BASES], bf16)
        rel_id = sb(part, "rel_id", [P, 1], f32)
        pid = sb(part, "pid", [P, 1], f32)
        pid_i = sb(part, "pid_i", [P, 2], i32)
        col_id = sb(part, "col_id", [P, P], f32)
        win_f = sb(part, "win_f", [1, CHUNKS], f32)
        tmp_a = sb(part, "tmp_a", [P, CHUNKS], f32)
        tmp_b = sb(part, "tmp_b", [P, CHUNKS], f32)
        tmp_i = sb(part, "tmp_i", [P, CHUNKS], i32)
        inside = sb(part, "inside", [P, 1], f32)
        part.close()
        part = ExitStack()
        gath = sb(part, "gath", [P, RING, FEAT], f32)
        idx = sb(part, "idx", [P, 4, QUAD], i32)
        spread = sb(part, "spread", [P, 2, QUAD, BASES, WIN], f32)
        hit = sb(part, "hit", [P, 2, QUAD, WIN], f32)
        part.close()
        coef_scope.close()
        part = ExitStack()
        cnt = sb(part, "cnt", [P, BLOCKS, DSTP], u16)
        base_t = sb(part, "base_t", [P, KIN, FEAT], f32)
        xt = sb(part, "xt", [P, 2, FEAT], f32)
        hot_s = sb(part, "hot_s", [P, QUAD, P], f16)
        hot_d = sb(part, "hot_d", [P, QUAD, AWIN], f16)
        zero_t = sb(part, "zero_t", [P, ZROW], f32)
        att = sb(part, "att", [P, 2, QUAD, ROW], f32)
        part.close()
        z_scope.close()
        sort_t = cnt[:, :, :].rearrange("p s d -> p (s d)").bitcast(f32)
        run_sum, place, blk_f, slot_f, blk_i, in_blk = (sort_t[:, CHUNKS * i:CHUNKS * (i + 1)] for i in range(6))
        blk_i, in_blk = blk_i.bitcast(i32), in_blk[:, 0:CHUNKS // 2].bitcast(bf16)
        x_low = [xt[:, 0, :], xt[:, 1, :]] + [z[:, 2, m, 0:FEAT] for m in range(2, 5)]
        bias0 = z[:, 2, 5, 0:FEAT]
        deg_part = [z[:, 3, 0, 0:HALF * P], z[:, 3, 1, 0:NODES - HALF * P]]
        x_high = [z[:, 0, j, 0:FEAT] for j in range(5)]

        late = ExitStack()
        adj = sb(late, "adj", [P, BLOCKS, NODES], f32)
        xs = sb(late, "xs", [P, BLOCKS, FEAT], f32)
        hs = sb(late, "hs", [P, BLOCKS, FEAT], f32)
        gt = sb(late, "gt", [P, KIN, NODES], f32)
        ht = sb(late, "ht", [P, KIN, NODES], f32)
        wa = sb(late, "wa", [P, KIN, FEAT], f32)
        wb = sb(late, "wb", [P, KIN, FEAT], f32)
        b_a = sb(late, "b_a", [P, FEAT], f32)
        b_b = sb(late, "b_b", [P, FEAT], f32)
        low = sb(late, "low", [P, 2, FEAT], f32)
        deg = sb(late, "deg", [P, BLOCKS], f32)
        dis = sb(late, "dis", [P, BLOCKS], f32)
        inv = sb(late, "inv", [P, BLOCKS], f32)
        seg_i = sb(late, "seg_i", [1, GROUPS], i32)
        seg_f = sb(late, "seg_f", [1, GROUPS], f32)
        seg_g = sb(late, "seg_g", [1, GROUPS], f32)
        at = sb(late, "at", [P, 2, QUAD, 2, 2 * ROW], f32)
        u = sb(late, "u", [P, QUAD, QUAD, P], f32)
        py = sb(late, "py", [P, 2, QUAD, 2 * HID], f32)
        vy = sb(late, "vy", [P, QUAD, 3, HID], f32)
        v_sum = sb(late, "v_sum", [P, QUAD, HID], f32)
        sw = sb(late, "sw", [P, QUAD, HID], f32)
        msg = sb(late, "msg", [P, 2, QUAD, MSG], f32)
        hot = sb(late, "hot", [P, 2, QUAD, P], f32)
        yr = sb(late, "yr", [P, 2, QUAD * QUAD, 4], f32)
        src_of = sb(late, "src_of", [P, 2, QUAD * QUAD, 1], f32)
        at_t = sb(late, "at_t", [P, QUAD * P], f32)
        soft = sb(late, "soft", [P, 2, QUAD * P], f32)
        hid = sb(late, "hid", [P, 2, QUAD * P], f32)
        iota_h = sb(late, "iota_h", [P, P], f32)
        w1_blk = sb(late, "w1_blk", [P, P], f32)
        w2_blk = sb(late, "w2_blk", [P, QUAD * P], f32)
        b1_c = sb(late, "b1_c", [P, 1], f32)
        b2_f = sb(late, "b2_f", [3, 2, P], f32)
        b2_r = sb(late, "b2_r", [3, P], bf16)
        b2_p = sb(late, "b2_p", [3, 3, P], bf16)
        ws_t = sb(late, "ws_t", [P, HID], f32)
        wv_t = sb(late, "wv_t", [P, HID], f32)
        late.close()
        agg = gt[:, :, :].rearrange("p k n -> p (k n)")[:, 0:BLOCKS * MSG]
        flat = ht[:, :, :].rearrange("p k n -> p (k n)")
        os_t, ov_t, qs_t, qv_t = (flat[:, P * i:P * (i + 1)] for i in range(4))
        agg_t = flat[:, 4 * P:8 * P].rearrange("p (a j n) -> p a j n", a=2, j=2)
        sv_t = flat[:, 10 * P:18 * P].rearrange("p (a j n) -> p a j n", a=2, j=4)
        ssp = flat[:, 18 * P:24 * P].rearrange("p (a j n) -> p a j n", a=2, j=3)

        ps = [ctx.enter_context(nc.psum_tensor(f"ps{i}", [P, 512], f32)) for i in range(8)]

        def semaphores(names):
            return [sem(n) for n in names.split()]

        ld_tab, ld_wc, ld_bias, st_h, st_zero, ld_w12, st_u, ld_mp, ld_mq, ld_x1 = semaphores(
            "ld_tab ld_wc ld_bias st_h st_zero ld_w12 st_u ld_mp ld_mq ld_x1")
        ld_x = semaphores("ld_x0 ld_x1a ld_x2")
        ld_et = semaphores("ld_et0 ld_et1 ld_et2 ld_et3")
        ld_base = semaphores("ld_base0 ld_base1 ld_base2 ld_base3")
        ld_xl, ld_xz, ld_xh, st_x = semaphores("ld_xl ld_xz ld_xh st_x")
        ld_att, st_att = semaphores("ld_att0 ld_att1"), semaphores("st_att0 st_att1")
        ld_at = semaphores("ld_at0 ld_at1")
        st_o = semaphores("st_o0 st_o1")
        gathered = [sem(f"gathered{i}") for i in range(RING)]
        u_in = [sem(f"u_in{i}") for i in range(QUAD)]
        const, zero_ok, cnt_in, hit_ok, g_o, ga_o, z_zero, z_zero_a, et_hot, win_out, win_pe, cnt_pe, coef_pe, coef_ok, fit_ok = semaphores(
            "const zero_ok cnt_in hit_ok g_o ga_o z_zero z_zero_a et_hot win_out win_pe cnt_pe coef_pe coef_ok fit_ok")
        ln_stat, ln_std, ln_rs, ln_h = semaphores("ln_stat ln_std ln_rs ln_h")
        idx_ok, spread_ok, z_pe, z_add = semaphores("idx_ok spread_ok z_pe z_add")
        g_idx, g_gath, g_spread, g_pe, g_add, edges_done = semaphores(
            "g_idx g_gath g_spread g_pe g_add edges_done")
        in_ok, rank_pe, rank_ok, cnt_zero = semaphores("in_ok rank_pe rank_ok cnt_zero")
        hot_ok, a_pe, a_add, ga_hot, ga_pe, ga_add, cnt_done = semaphores(
            "hot_ok a_pe a_add ga_hot ga_pe ga_add cnt_done")
        tile_pe, half_pe, o_free, o_done, att_ok = semaphores(
            "tile_pe half_pe o_free o_done att_ok")
        adj_act, adj_ok, deg_pe, deg_ok, deg_sq, agg_pe, gt_ok, lin_pe, lin_ok, act_h = semaphores(
            "adj_act adj_ok deg_pe deg_ok deg_sq agg_pe gt_ok lin_pe lin_ok act_h")
        u_pe, u_ev, t_pe, t_act, h_pe, h_act, h_ok, w_pe, y_ok, p_ok, v_ok, m_ok, m_pe, m_add, pre_ok = semaphores(
            "u_pe u_ev t_pe t_act h_pe h_act h_ok w_pe y_ok p_ok v_ok m_ok m_pe m_add pre_ok")
        q_t, q_ev, q_o, q_act, q_ok, q_pe, q_x = semaphores("q_t q_ev q_o q_act q_ok q_pe q_x")
        dve_o, act_o = semaphores("dve_o act_o")

        ld_w3, ld_w4 = semaphores("ld_w3 ld_w4")
        COUNTS = (HALF + 1, HALF + 1)
        LOW_COUNTS = (BASES * KIN - BLOCKS) * COUNTS[0]
        assert LOW_COUNTS % QUAD == 0 and CHUNKS - LOW_COUNTS <= BASES * KIN * COUNTS[1]
        REAL_QUADS = -(-REAL_CHUNKS // QUAD)
        ATT_DONE = [16 * len([t for t in range(REAL_CHUNKS) if t // QUAD % 2 == par]) for par in range(2)]

        def steps(eng, n, first, last, body, skip=0):
            for i in range(skip, first):
                body(i)
            with eng.Fori(first, n - last) as i:
                body(i)
            for i in range(n - last, n):
                body(i)

        def valid(st):
            return not isinstance(st, int) or 0 <= st < STEPS

        def message_steps(eng, body):
            for st in range(-QUAD, 8):
                body(st, st // QUAD, st % 2, st % 8)
            with eng.Fori(1, STEPS // 8) as i:
                for s8 in range(8):
                    body(i * 8 + s8, i * 2 + s8 // QUAD, s8 % 2, s8)
            for st in range(STEPS // 8 * 8, STEPS):
                body(st, st // QUAD, st % 2, st % 8)

        def more(r):
            return not isinstance(r, int) or r < RADIALS

        def loaded(r, rpar):
            return (r - rpar) * 8 + 16

        def lap16(st, s):
            return 2 * (st - s) + 16 * (s // 8) + 16

        def in_reg(eng, value):
            return value if isinstance(value, int) else eng.to_reg(value)

        def after(eng, s, value):
            if not isinstance(value, int) or value > 0:
                eng.wait_ge(s, value)

        block = ctx.enter_context(nc.Block())

        @block.sync
        def _(sp):
            sp.dma_start(dst_i[:, :], dst).then_inc(ld_tab, 16)
            sp.dma_start(src_i[:, :], src).then_inc(ld_tab, 16)
            sp.dma_start(norm_f[:, :], norm).then_inc(ld_tab, 16)
            for s, (a, b) in zip(ld_x, ((0, 4), (4, 9))):
                sp.dma_start(x_in[:, a:b, :], x[a * P:b * P, :].rearrange("(n p) f -> p n f", p=P)).then_inc(s, 16)
            sp.dma_start(x_in[0:LAST, 9, :], x[9 * P:NODES, :]).then_inc(ld_x[2], 16)
            sp.wait_ge(const, 1)
            for q in range(QUAD):
                sp.dma_start(wc_blk[RELS * q:RELS * (q + 1), BASES * q:BASES * (q + 1)], w_comp).then_inc(ld_wc, 16)
            for j in range(CHUNKS // QUAD // ETS):
                if j >= 4:
                    sp.wait_ge(et_hot, j - 3)
                for q in range(QUAD):
                    sp.dma_start(et_i[RELS * q:RELS * (q + 1), j % 4, :],
                                 etype[q:q + 1, j * ETS * P:(j + 1) * ETS * P].to_broadcast([RELS, ETS * P]))\
                        .then_inc(ld_et[j % 4], 16)
            sp.wait_ge(zero_ok, 1)
            for i in range(FILLS):
                sp.wait_ge(tile_pe, i + 1)
                sp.dma_start(slots[i * SLOTS // FILLS:(i + 1) * SLOTS // FILLS, :].rearrange(
                                 "(p a r) c -> p a (r c)", p=P, r=ZROW // ROW),
                             zero_t[:, :].unsqueeze(1).broadcast_to([P, SLOTS * ROW // P // FILLS // ZROW, ZROW]))\
                    .then_inc(st_zero, 16)
            sp.wait_ge(edges_done, 1)

            def attributes(g, par, lap):
                after(sp, st_att[par], 16 * QUAD * lap)
                sp.dma_start(att[:, par, :, :], attr[:, bass.ds(g * QUAD, QUAD), :]).then_inc(ld_att[par], 16)

            def attribute_pair(i):
                for par in range(2):
                    attributes(2 * i + par, par, i)

            steps(sp, REAL_QUADS // 2, 1, 0, attribute_pair)
            attributes(REAL_QUADS - 1, (REAL_QUADS - 1) % 2, REAL_QUADS // 2)
            sp.wait_ge(adj_ok, 1)
            for par in range(2):
                sp.wait_ge(st_att[par], ATT_DONE[par])
            sp.wait_ge(cnt_zero, 2)
            for c in range(QUAD):
                h = slice(HID * c, HID * (c + 1))
                sp.dma_start(w1_blk[HID * c:HID * c + RAD, h], m_w1).then_inc(ld_mp, 16)
                sp.dma_start(w2_blk[h, P * c:P * (c + 1)], m_w2).then_inc(ld_mp, 16)
                sp.dma_start(b1_c[h, :], m_b1).then_inc(ld_mp, 16)
            sp.dma_start(b2_f[:, 0, :], m_b2.to_broadcast([3, P])).then_inc(ld_mp, 16)
            sp.dma_start(ws_t[:, :], m_ws).then_inc(ld_mp, 16)
            sp.dma_start(wv_t[:, :], m_wv).then_inc(ld_mp, 16)

            def sorted_quad(qn, par):
                if not isinstance(qn, int) or qn >= 2:
                    sp.wait_ge(u_in[QUAD - 1], 64 * (qn - 1))
                    sp.wait_ge(t_pe, qn - 1)
                    sp.wait_ge(y_ok, qn - 1)
                sp.dma_start(at[:, par, :, :, :].rearrange("p s g w -> p (s g) w"),
                             slots[bass.ds(qn * QUAD * 2 * GROUP, QUAD * 2 * GROUP), :].rearrange(
                                 "(s p c) w -> p s (c w)", p=P, c=2)).then_inc(ld_at[par], 16)

            for qn in range(2):
                sorted_quad(qn, qn)
            sp.wait_ge(u_ev, BLOCKS)
            sp.dma_start(os_t[0:2 * HID, :], m_os).then_inc(ld_mq, 16)
            for i in range(2):
                sp.dma_start(ov_t[2 * HID * i:2 * HID * (i + 1), :], m_ov).then_inc(ld_mq, 16)
            sp.dma_start(qs_t, m_qs).then_inc(ld_mq, 16)
            sp.dma_start(qv_t, m_qv).then_inc(ld_mq, 16)
            sp.wait_ge(lin_ok, 2 * BLOCKS)
            for t, w in ((wa, s_w1l), (wb, s_w1r)):
                sp.dma_start(t[:, :, :], w.rearrange("(k p) f -> p k f", p=P)).then_inc(ld_w3, 16)
            for t, w in ((b_a, s_b1), (b_b, s_b2)):
                sp.dma_start(t[:, :], w.to_broadcast([P, FEAT])).then_inc(ld_w3, 16)

            def sorted_pair(i):
                for par in range(2):
                    sorted_quad(2 * i + par, par)

            steps(sp, STEPS // QUAD // 2, 1, 0, sorted_pair, skip=1)
            sorted_quad(STEPS // QUAD - 1, 0)
            sp.wait_ge(lin_ok, 4 * BLOCKS)
            for t, w in ((wa, s_w2l), (wb, s_w2r)):
                sp.dma_start(t[:, :, :], w.rearrange("(k p) f -> p k f", p=P)).then_inc(ld_w4, 16)
            for n in range(BLOCKS):
                sp.wait_ge(lin_ok, 4 * BLOCKS + 2 * (n + 1))
                sp.dma_start(out[n * P:n * P + rows(n), :], low[0:rows(n), n % 2, :]).then_inc(st_o[n % 2], 16)
            for par in range(2):
                sp.wait_ge(st_o[par], 16 * BLOCKS // 2)

        @block.scalar
        def _(act):
            def ln_std_of(k, n):
                r = rows(n)
                act.wait_ge(ln_stat, BLOCKS * k + n + 1)
                nc.scalar.activation(std[0:r, n:n + 1], mv[0:r, n, 1:2], ACT.Sqrt, bias=epsb[0:r, :]).then_inc(ln_std, 1)

            def ln_h_of(k, n, src_t, dst_t):
                r = rows(n)
                act.wait_ge(ln_rs, BLOCKS * k + n + 1)
                nc.scalar.activation(dst_t[0:r, n, :], src_t[0:r, n, :], ACT.Relu, bias=nmr[0:r, n:n + 1],
                                     scale=rstd[0:r, n:n + 1]).then_inc(ln_h, 1)

            def layernorm(k, src_t, dst_t):
                for n in range(BLOCKS + 1):
                    if n < BLOCKS:
                        ln_std_of(k, n)
                    if n:
                        ln_h_of(k, n - 1, src_t, dst_t)

            act.wait_ge(const, 1)
            layernorm(0, x_in, x_in)
            for n in range(BLOCKS):
                act.wait_ge(ln_h, n + 1)
                act.dma_start(h_rows[n * P:n * P + rows(n), :], x_in[0:rows(n), n, :]).then_inc(st_h, 16)
            act.wait_ge(z_zero, 1)
            act.wait_ge(st_h, 16 * BLOCKS)
            nc.scalar.activation(zk[3], zk[0], ACT.Copy).then_inc(z_zero_a, 1)
            act.wait_ge(edges_done, 1)
            for m in range(2):
                act.dma_start(x_low[m], x[m * P:(m + 1) * P, :]).then_inc(ld_xl, 16)

            def base_tile(use, k):
                if use:
                    act.wait_ge(tile_pe, (use - 1) * KIN + k + 1)
                act.dma_start(base_t[:, k, :], bases[use % BASES, k * P:(k + 1) * P, :]).then_inc(ld_base[k], 16)

            for use in range(BASES + 1):
                for k in range(KIN):
                    base_tile(use, k)
            act.wait_ge(half_pe, 1)
            for m in range(2, HALF):
                act.dma_start(x_low[m], x[m * P:(m + 1) * P, :]).then_inc(ld_xz, 16)
            act.dma_start(bias0, h_bias.to_broadcast([P, FEAT])).then_inc(ld_bias, 16)
            for m in range(HALF, BLOCKS):
                act.dma_start(x_high[m - HALF][0:rows(m), :], x[m * P:m * P + rows(m), :]).then_inc(ld_xh, 16)
            for m in range(HALF):
                act.wait_ge(o_done, m + 1)
                act.dma_start(x1_rows[m * P:(m + 1) * P, :], x_low[m]).then_inc(st_x, 16)
            for use in range(BASES + 1, 2 * BASES):
                for k in range(KIN):
                    base_tile(use, k)
            act.wait_ge(st_x, 16 * HALF)
            act.wait_ge(half_pe, 2)
            act.dma_start(xs[:, 0:HALF, :], x1_rows.rearrange("(n p) f -> p n f", p=P)).then_inc(ld_x1, 16)
            for t, w in ((wa, g_w1), (wb, g_w2)):
                act.dma_start(t[:, :, :], w.rearrange("(k p) f -> p k f", p=P)).then_inc(ld_w12, 16)
            for t, w in ((b_a, g_b1), (b_b, g_b2)):
                act.dma_start(t[:, :], w.to_broadcast([P, FEAT])).then_inc(ld_w12, 16)
            act.wait_ge(cnt_done, 1)
            for s in range(5, BLOCKS):
                nc.scalar.activation(adj[:, s, :], cnt[:, s, 0:NODES], ACT.Copy).then_inc(adj_act, 1)
            act.wait_ge(deg_ok, 1)
            nc.scalar.activation(dis[:, :], deg[:, :], ACT.Sqrt, bias=1.0).then_inc(deg_sq, 1)
            layernorm(1, xs, hs)

            n_agg, n_gt, n_h = Count(), Count(), Count()

            def evacuate_transposed(r, n):
                act.wait_ge(agg_pe, n_agg.n + 1)
                bank = ps[n_agg.n % 4]
                n_agg.up()
                nc.scalar.activation(ht[:, :, n * P:n * P + r],
                                     bank[:, :].rearrange("p (k c) -> p k c", k=KIN)[:, :, 0:r], ACT.Copy)\
                    .then_inc(gt_ok, n_gt.up())

            def evacuate_aggregated():
                for a, b in COLS:
                    for k in range(KIN):
                        act.wait_ge(agg_pe, n_agg.n + 1)
                        bank = ps[n_agg.n % 4]
                        n_agg.up()
                        nc.scalar.activation(gt[:, k, a:b], bank[:, 0:b - a], ACT.Copy).then_inc(gt_ok, n_gt.up())

            evacuate_aggregated()
            for n in range(BLOCKS):
                r = rows(n)
                act.wait_ge(lin_ok, n + 1)
                nc.scalar.activation(hs[0:r, n, :], low[0:r, n % 2, :], ACT.Relu, scale=dis[0:r, n:n + 1])\
                    .then_inc(act_h, n_h.up())
            evacuate_aggregated()
            layernorm(2, xs, hs)
            scale_b = P ** -0.5
            for n in range(BLOCKS + 1):
                if n < BLOCKS:
                    evacuate_transposed(rows(n), n)
                if n:
                    r = rows(n - 1)
                    act.wait_ge(u_pe, n)
                    nc.scalar.activation(u[0:r, (n - 1) // 4, (n - 1) % 4, :], ps[4 + (n - 1) % 2][0:r, 0:P], ACT.Copy,
                                         scale=scale_b).then_inc(u_ev, 1)
                    act.wait_ge(u_ev, n)
                    act.dma_start(u_rows[(n - 1) * P:(n - 1) * P + r, :], u[0:r, (n - 1) // 4, (n - 1) % 4, :])\
                        .then_inc(st_u, 16)

            def radial(st, r, par, s8):
                if valid(st + 1):
                    rn, rpar = (r + (s8 + 1) // QUAD - s8 // QUAD, (s8 + 1) // QUAD % 2)
                    act.wait_ge(w_pe, st + 2)
                    act.wait_ge(y_ok, rn + 1)
                    after(act, m_ok, st)
                    for c in range(QUAD):
                        q = (s8 + 1) % QUAD * QUAD + c
                        last = nc.scalar.activation(py[:, 1 - par, c, :], ps[1 - par][:, c * P:c * P + 2 * HID],
                                                    ACT.Copy, scale=yr[:, rpar, q, 0:1])
                    last.then_inc(p_ok, 1)
                if more(r + 1) and s8 % QUAD == 0:
                    act.wait_ge(t_pe, r + 2)
                    after(act, h_pe, r + 1)
                    nc.scalar.activation(at_t[:, :], ps[2][:, :], ACT.Copy).then_inc(t_act, 1)
                if more(r + 1) and s8 % QUAD == 1:
                    act.wait_ge(h_pe, r + 2)
                    after(act, h_ok, r + 1)
                    nc.scalar.activation(soft[:, 0, :], ps[3][:, :], ACT.Abs, bias=b1_c[:, :]).then_inc(act_o, 1)
                    nc.scalar.activation(soft[:, 1, :], ps[3][:, :], ACT.Relu, bias=b1_c[:, :])
                    act.wait_ge(act_o, 2 * (r + 1) + 1)
                    nc.scalar.activation(soft[:, 0, :], soft[:, 0, :], ACT.Exp, scale=-1.0).then_inc(act_o, 1)
                if more(r + 1) and s8 % QUAD == 2:
                    act.wait_ge(act_o, 2 * (r + 1) + 2)
                    nc.scalar.activation(soft[:, 0, :], soft[:, 0, :], ACT.Ln, bias=1.0).then_inc(h_act, 1)

            act.wait_ge(ld_mp, 16 * 15)
            message_steps(act, radial)
            act.wait_ge(ld_mq, 16 * 5)
            scale_f = (2 * HID) ** -0.5
            for n in range(-2, BLOCKS):
                if n + 2 < BLOCKS:
                    m = n + 2
                    r = rows(m)
                    act.wait_ge(q_t, m + 1)
                    after(act, q_o, m - 1)
                    nc.scalar.activation(agg_t[:, m % 2, :, 0:r],
                                         ps[m % 2][:, 0:2 * P].rearrange("p (j n) -> p j n", j=2)[:, :, 0:r], ACT.Copy)\
                        .then_inc(q_ev, 1)
                if 0 <= n + 1 < BLOCKS:
                    m = n + 1
                    r = rows(m)
                    bank = ps[2 + m % 2]
                    act.wait_ge(q_o, m + 1)
                    after(act, q_pe, m - 1)
                    nc.scalar.activation(ssp[:, m % 2, 0, 0:r], bank[:, 0:r], ACT.Abs, scale=scale_f).then_inc(act_o, 1)
                    nc.scalar.activation(ssp[:, m % 2, 2, 0:r], bank[:, 0:r], ACT.Relu, scale=scale_f)
                    for c in range(3):
                        nc.scalar.activation(sv_t[:, m % 2, c + 1, 0:r],
                                             (bank if c % 2 else ps[6 + m % 2])[:, (c + 1) * P:(c + 1) * P + r],
                                             ACT.Copy, scale=scale_f)
                    act.wait_ge(act_o, 2 * RADIALS + 2 * m + 1)
                    nc.scalar.activation(ssp[:, m % 2, 1, 0:r], ssp[:, m % 2, 0, 0:r], ACT.Exp, scale=-1.0).then_inc(act_o, 1)
                    act.wait_ge(act_o, 2 * RADIALS + 2 * m + 2)
                    nc.scalar.activation(ssp[:, m % 2, 0, 0:r], ssp[:, m % 2, 1, 0:r], ACT.Ln, bias=1.0).then_inc(q_act, 1)
            layernorm(3, xs, hs)
            for lay in range(2):
                for n in range(BLOCKS):
                    evacuate_transposed(rows(n), n)
                evacuate_aggregated()
                if lay == 0:
                    for n in range(BLOCKS):
                        r = rows(n)
                        act.wait_ge(lin_ok, 2 * BLOCKS + 2 * (n + 1))
                        nc.scalar.activation(hs[0:r, n, :], low[0:r, n % 2, :], ACT.Tanh).then_inc(act_h, n_h.up())

        @block.gpsimd
        def _(pool):
            nc.gpsimd.iota(pid_i[:, 0:1], pattern=[[0, 1]], base=0, channel_multiplier=1)
            nc.gpsimd.iota(pid[:, :], pattern=[[0, 1]], base=0, channel_multiplier=1,
                           allow_small_or_imprecise_dtypes=True)
            nc.gpsimd.iota(col_id[:, :], pattern=[[1, P]], base=0, channel_multiplier=0,
                           allow_small_or_imprecise_dtypes=True)
            nc.gpsimd.iota(iota_a[:, :], pattern=[[1, AWIN]], base=0, channel_multiplier=0,
                           allow_small_or_imprecise_dtypes=True)
            nc.gpsimd.iota(iota_w[:, :], pattern=[[1, WIN]], base=0, channel_multiplier=0,
                           allow_small_or_imprecise_dtypes=True)
            nc.gpsimd.memset(ones[:, :], 1.0)
            nc.gpsimd.memset(ones_b[:, :], 1.0)
            nc.gpsimd.memset(epsb[:, :], EPS)
            nc.gpsimd.memset(slot_i[:, :], 0)
            nc.gpsimd.memset(wc_blk[:, :], 0.0).then_inc(const, 1)
            nc.gpsimd.memset(zk[0], 0.0).then_inc(z_zero, 1)
            nc.gpsimd.memset(zk[1], 0.0).then_inc(z_zero, 1)
            nc.gpsimd.memset(zk[2], 0.0).then_inc(z_zero, 1)
            pool.wait_ge(st_h, 16 * BLOCKS)
            pool.wait_ge(fit_ok, 1)
            pool.wait_ge(coef_ok, SLICES)

            def gather_ring(i, par, skip, chunks=RING):
                for c in range(chunks):
                    if c % QUAD == 0:
                        nc.gpsimd.tensor_copy(idx[:, 2 * par + c // QUAD, :],
                                              src_i[:, bass.ds(i * 2 * RING + par * RING + c, QUAD)]).then_inc(idx_ok, 1)
                    indexed = in_reg(pool, i * 4 + 2 * par + c // QUAD + 1)
                    used = in_reg(pool, i * 2 * RING + par * RING + c - RING + 1)
                    pool.wait_ge(fit_ok, 1)
                    if not skip:
                        pool.wait_ge(z_pe, used)
                    pool.wait_ge(idx_ok, indexed)
                    nc.gpsimd.indirect_dma_start(
                        out=gath[:, c, :], out_offset=None, in_=h_rows,
                        in_offset=bass.IndirectOffsetOnAxis(ap=idx[:, 2 * par + c // QUAD, c % QUAD:c % QUAD + 1], axis=0))\
                        .then_inc(gathered[c], 16)

            with pool.If(pool.value_load(fits[0:1, 0:1], min_val=0, max_val=1) == 1):
                for par in range(2):
                    gather_ring(0, par, par == 0)
                with pool.Fori(1, REAL_CHUNKS // RING // 2) as i:
                    for par in range(2):
                        gather_ring(i, par, False)
                gather_ring(REAL_CHUNKS // RING // 2, 0, False)
                gather_ring(REAL_CHUNKS // RING // 2, 1, False, REST)
            with pool.Else():
                with pool.Fori(0, REAL_CHUNKS) as c:
                    used = in_reg(pool, c * WINDOWS + 1)
                    pool.wait_ge(fit_ok, 1)
                    pool.wait_ge(g_add, used)
                    nc.gpsimd.tensor_copy(idx[:, 0, 0:1], src_i[:, bass.ds(c, 1)]).then_inc(g_idx, 1)
                    indexed = in_reg(pool, c + 1)
                    pool.wait_ge(fit_ok, 1)
                    pool.wait_ge(g_idx, indexed)
                    nc.gpsimd.indirect_dma_start(
                        out=gath[:, 0, :], out_offset=None, in_=h_rows,
                        in_offset=bass.IndirectOffsetOnAxis(ap=idx[:, 0, 0:1], axis=0)).then_inc(g_gath, 16)
            pool.wait_ge(edges_done, 1)
            nc.gpsimd.memset(zero_t[:, :], 0.0).then_inc(zero_ok, 1)
            pool.wait_ge(rank_ok, 1)
            nc.gpsimd.memset(cnt[:, :, :].rearrange("p s d -> p (s d)").bitcast(i32), 0).then_inc(cnt_zero, 1)

            pool.wait_ge(st_zero, 16 * FILLS)

            def scatter_quad(g, par, lap, tail):
                at_i = att[:, par, :, :].bitcast(i32)
                loaded, copied = in_reg(pool, lap * 16 + 16), in_reg(pool, g + 1)
                pool.wait_ge(rank_ok, 1)
                pool.wait_ge(ld_att[par], loaded)
                nc.gpsimd.tensor_copy(at_i[:, :, DSTC:DSTC + 1], dst_i[:, bass.ds(g * QUAD, QUAD)].unsqueeze(2))
                nc.gpsimd.tensor_copy(att[:, par, :, SRCC:SRCC + 1], srclo[:, bass.ds(g * QUAD, QUAD)].unsqueeze(2))
                nc.gpsimd.tensor_copy(idx_s[:, par, :], slot_i[:, bass.ds(g * QUAD, QUAD)]).then_inc(att_ok, 1)
                pool.wait_ge(st_zero, 16 * FILLS)
                pool.wait_ge(att_ok, copied)
                for c in range(1 if tail else QUAD):
                    r = TAIL if tail else P
                    nc.gpsimd.indirect_dma_start(
                        out=slots, out_offset=bass.IndirectOffsetOnAxis(ap=idx_s[0:r, par, c:c + 1], axis=0),
                        in_=att[0:r, par, c, :], in_offset=None).then_inc(st_att[par], 16)

            def scatter_pair(i):
                for par in range(2):
                    scatter_quad(2 * i + par, par, i, False)

            with pool.Fori(0, REAL_QUADS // 2) as i:
                scatter_pair(i)
            scatter_quad(REAL_QUADS - 1, (REAL_QUADS - 1) % 2, REAL_QUADS // 2, True)
            pool.wait_ge(adj_ok, 1)
            for par in range(2):
                pool.wait_ge(st_att[par], ATT_DONE[par])
            nc.gpsimd.iota(iota_h[:, :], pattern=[[1, P]], base=0, channel_multiplier=0,
                           allow_small_or_imprecise_dtypes=True)
            nc.gpsimd.memset(w1_blk[:, :], 0.0)
            nc.gpsimd.memset(w2_blk[:, :], 0.0).then_inc(cnt_zero, 1)
            pool.wait_ge(st_u, 16 * BLOCKS)

            def gather_dst(st, par, s8):
                if not valid(st):
                    return
                there, used = in_reg(pool, lap16(st, s8)), in_reg(pool, st - QUAD + 1)
                pool.wait_ge(st_u, 16 * BLOCKS)
                pool.wait_ge(ld_at[s8 // QUAD], there)
                after(pool, m_ok, used)
                at_i = at[:, s8 // QUAD, s8 % QUAD, :, :].rearrange("p g (c w) -> p (g c) w", c=2).bitcast(i32)
                for c in range(QUAD):
                    nc.gpsimd.indirect_dma_start(
                        out=u[:, s8 % QUAD, c, :], out_offset=None, in_=u_rows,
                        in_offset=bass.IndirectOffsetOnAxis(ap=at_i[:, c, DSTC:DSTC + 1], axis=0))\
                        .then_inc(u_in[s8 % QUAD], 16)

            for st in range(8):
                gather_dst(st, st % 2, st % 8)
            with pool.Fori(1, STEPS // 8) as i:
                for s8 in range(8):
                    gather_dst(i * 8 + s8, s8 % 2, s8)
            for st in range(STEPS // 8 * 8, STEPS):
                gather_dst(st, st % 2, st % 8)

        @block.tensor
        def _(pe):
            mm = nc.tensor.matmul
            pe.wait_ge(const, 2)
            pe.wait_ge(win_out, 1)
            mm(ps[5][:, 0:CHUNKS], ones[0:1, :], win_f[0:1, :], start=True, stop=True).then_inc(win_pe, 1)
            pe.wait_ge(cnt_in, 1)
            mm(ps[6][0:1, 0:1], inside[:, 0:1], ones[:, 0:1], start=True, stop=True).then_inc(cnt_pe, 1)
            for j in range(CHUNKS // QUAD // ETS):
                pe.wait_ge(et_hot, j + 1)
                if j >= 5:
                    pe.wait_ge(coef_ok, j - 4)
                for g in range(ETS):
                    for i in range(3):
                        last = mm(ps[j % 5][:, g * QUAD * BASES:(g + 1) * QUAD * BASES],
                                  et_1[:, j % 2, g * P:(g + 1) * P], wc_part[:, i, :], start=(i == 0), stop=(i == 2))
                last.then_inc(coef_pe, 1)
            pe.wait_ge(fit_ok, 1)
            pe.wait_ge(coef_ok, SLICES)
            fit = pe.value_load(fits[0:1, 0:1], min_val=0, max_val=1)

            def add_edges(bank, h_slot, s_of):
                for k in range(KIN):
                    last = mm(bank[:, k * P:(k + 1) * P], gath[:, h_slot, k * P:(k + 1) * P],
                              s_of.rearrange("p b d -> p (b d)"), start=True, stop=True)
                return last

            def edge_ring(i, first, chunks=RING):
                for slot in range(chunks):
                    if slot % QUAD == 0:
                        pe.wait_ge(spread_ok, i * 2 + slot // QUAD + 1)
                    pe.wait_ge(gathered[slot], i * 16 + 16)
                    if not first:
                        pe.wait_ge(z_add, i * RING + slot - RING + 2)
                    add_edges(ps[slot], slot, spread[:, slot // QUAD, slot % QUAD, :, :]).then_inc(z_pe, 1)

            with pe.If(fit == 1):
                edge_ring(0, True)
                with pe.Fori(1, REAL_CHUNKS // RING) as i:
                    edge_ring(i, False)
                edge_ring(REAL_CHUNKS // RING, False, REST)
            with pe.Else():
                with pe.Fori(0, REAL_CHUNKS) as c:
                    with pe.Fori(0, WINDOWS) as k:
                        pe.wait_ge(g_gath, c * 16 + 16)
                        pe.wait_ge(g_spread, c * WINDOWS + k + 1)
                        add_edges(ps[0], 0, spread[:, 0, 0, :, :]).then_inc(g_pe, 1)

            def rank(k):
                pe.wait_ge(in_ok, k + 1)
                mm(ps[5][:, 0:CHUNKS], below[:, :], in_blk, start=True, stop=True)
                mm(ps[6][:, 0:CHUNKS], ones_b[:, :], in_blk, start=True, stop=True).then_inc(rank_pe, 1)

            def count(t):
                pe.wait_ge(hot_ok, t + 1)
                if t >= 2:
                    pe.wait_ge(a_add, t)
                mm(ps[5 + t % 2][:, 0:AWIN], hot_s[:, t % QUAD, :], hot_d[:, t % QUAD, :], start=True, stop=True)\
                    .then_inc(a_pe, 1)

            def base_products(between):
                pe.wait_ge(edges_done, 1)
                for half in range(2):
                    for b in range(BASES):
                        for k in range(KIN):
                            use = half * BASES + b
                            pe.wait_ge(ld_base[k], 16 * (use + 1))
                            for j in range(HALF):
                                n = half * HALF + j
                                if half and b == 0 and k == 0:
                                    pe.wait_ge(o_free, j + 1)
                                last = mm(ps[j][0:rows(n), :], z[:, k, b, n * P:n * P + rows(n)], base_t[:, k, :],
                                          start=(b == 0 and k == 0), stop=(b == BASES - 1 and k == KIN - 1))
                                if j == HALF - 1:
                                    last.then_inc(tile_pe, 1)
                                between((use * KIN + k) * HALF + j)
                    mm(ps[7][0:1, 0:1], ones[:, 0:1], ones[:, 0:1], start=True, stop=True).then_inc(half_pe, 1)

            def rank_and_count(i):
                tile, j = i // HALF, i % HALF
                if tile < BLOCKS:
                    if j == HALF - 1:
                        rank(tile)
                    return
                half = tile // (BASES * KIN)
                t = LOW_COUNTS + (tile - BASES * KIN) * COUNTS[1] if half else (tile - BLOCKS) * COUNTS[0]
                for c in range(t + j * COUNTS[half] // HALF, t + (j + 1) * COUNTS[half] // HALF):
                    if c < REAL_CHUNKS:
                        count(c)

            with pe.If(fit == 1):
                base_products(rank_and_count)
            with pe.Else():
                for k in range(BLOCKS):
                    rank(k)
                with pe.Fori(0, REAL_CHUNKS) as c:
                    with pe.Fori(0, WINDOWS) as k:
                        pe.wait_ge(ga_hot, c * WINDOWS + k + 1)
                        mm(ps[5][:, 0:AWIN], hot_s[:, 0, :], hot_d[:, 0, :], start=True, stop=True).then_inc(ga_pe, 1)
                base_products(lambda i: None)

            pe.wait_ge(cnt_done, 1)
            for n in range(BLOCKS):
                r = rows(n)
                part_of, a = deg_part[n // HALF], n % HALF * P
                last = mm(ps[7][0:r, n:n + 1], part_of[:, a:a + r], ones[:, 0:1], start=True, stop=True)
            last.then_inc(deg_pe, 1)

            n_agg, n_lin = Count(), Count()

            def transpose_block(n):
                r = rows(n)
                after(pe, gt_ok, n_agg.n - 3)
                bank = ps[n_agg.n % 4]
                n_agg.up()
                for k in range(KIN):
                    last = nc.tensor.transpose(bank[:, k * P:k * P + r], hs[0:r, n, k * P:(k + 1) * P], ident[0:r, 0:r])
                last.then_inc(agg_pe, 1)

            def aggregate(h_sem, h_base):
                pe.wait_ge(adj_ok, 1)
                for j, (a, b) in enumerate(COLS):
                    for k in range(KIN):
                        after(pe, gt_ok, n_agg.n - 3)
                        bank = ps[n_agg.n % 4]
                        n_agg.up()
                        for s in range(BLOCKS):
                            if j == 0 and k == 0:
                                pe.wait_ge(h_sem, h_base + s + 1)
                            last = mm(bank[:, 0:b - a], hs[0:rows(s), s, k * P:(k + 1) * P], adj[0:rows(s), s, a:b],
                                      start=(s == 0), stop=(s == BLOCKS - 1))
                        last.then_inc(agg_pe, 1)

            def product(n, t, w):
                r = rows(n)
                after(pe, lin_ok, n_lin.n - 3)
                bank = ps[4 + n_lin.n % 4]
                n_lin.up()
                for k in range(KIN):
                    last = mm(bank[0:r, :], t[:, k, n * P:n * P + r], w[:, k, :], start=(k == 0), stop=(k == KIN - 1))
                last.then_inc(lin_pe, 1)

            def aggregated(n):
                end = n * P + rows(n)
                part_of = next(j for j, (a, b) in enumerate(COLS) if end <= b)
                pe.wait_ge(gt_ok, n_agg.n - (len(COLS) - 1 - part_of) * KIN)

            for conv in range(2):
                aggregate(ln_h if conv == 0 else act_h, BLOCKS if conv == 0 else 0)
                pe.wait_ge(ld_w12, 64)
                for n in range(BLOCKS):
                    aggregated(n)
                    product(n, gt, wa if conv == 0 else wb)

            pe.wait_ge(ld_mp, 16 * 15)
            for n in range(BLOCKS + 1):
                if n < BLOCKS:
                    pe.wait_ge(ln_h, 2 * BLOCKS + n + 1)
                    r = rows(n)
                    after(pe, gt_ok, n_agg.n - 3)
                    bank = ps[n_agg.n % 4]
                    n_agg.up()
                    nc.tensor.transpose(bank[:, 0:r], hs[0:r, n, 0:P], ident[0:r, 0:r])
                    for c in range(3):
                        last = nc.tensor.transpose(bank[:, (c + 1) * P:(c + 1) * P + r], hs[0:r, n, P + c:FEAT:3],
                                                   ident[0:r, 0:r])
                    last.then_inc(agg_pe, 1)
                if n:
                    m, r = n - 1, rows(n - 1)
                    pe.wait_ge(gt_ok, n_agg.n - (1 if n < BLOCKS else 0))
                    if m < 2:
                        pe.wait_ge(lin_ok, 2 * BLOCKS)
                    after(pe, u_ev, m - 1)
                    for j in range(4):
                        last = mm(ps[4 + m % 2][0:r, j * HID:(j + 1) * HID], ht[:, j, m * P:m * P + r],
                                  (ws_t if j == 0 else wv_t)[:, :], start=True, stop=True)
                    last.then_inc(u_pe, 1)
            pe.wait_ge(pre_ok, 2)

            def message(st, r, par, s8):
                if valid(st + 1):
                    rn, rpar = (r + (s8 + 1) // QUAD - s8 // QUAD, (s8 + 1) // QUAD % 2)
                    pe.wait_ge(h_ok, rn + 1)
                    after(pe, m_ok, st)
                    q = (s8 + 1) % QUAD
                    mm(ps[1 - par][:, :], ones_b[0:3, :], b2_r[:, :].unsqueeze(1).broadcast_to([3, QUAD, P]),
                       start=True, stop=False)
                    mm(ps[1 - par][:, :], hid[:, rpar, q * P:(q + 1) * P], w2_blk[:, :], start=False, stop=True)\
                        .then_inc(w_pe, 1)
                if more(r + 1) and s8 % QUAD == 0:
                    rpar = (s8 // QUAD + 1) % 2
                    pe.wait_ge(ld_at[rpar], loaded(r + 1, rpar))
                    after(pe, t_act, r + 1)
                    if isinstance(r, int) and r < 0:
                        pe.wait_ge(u_ev, BLOCKS)
                    for q in range(QUAD):
                        last = nc.tensor.transpose(ps[2][:, q * P:(q + 1) * P],
                                                   at[:, rpar, q, :, :].rearrange("p g w -> p (g w)"), ident[:, :])
                    last.then_inc(t_pe, 1)
                if more(r + 1) and s8 % QUAD == 1:
                    pe.wait_ge(t_act, r + 2)
                    after(pe, h_act, r + 1)
                    mm(ps[3][:, :], w1_blk[:, :], at_t[:, :], start=True, stop=True).then_inc(h_pe, 1)
                if valid(st):
                    pe.wait_ge(m_ok, st + 1)
                    for g in range(2):
                        after(pe, m_add, 2 * st + g - 3)
                        for c in range(2):
                            last = mm(ps[4 + 2 * par + g][:, 0:MSG], hot[:, par, 2 * g + c, :], msg[:, par, 2 * g + c, :],
                                      start=(c == 0), stop=(c == 1))
                        last.then_inc(m_pe, 1)

            message_steps(pe, message)
            pe.wait_ge(ld_mq, 16 * 5)
            pe.wait_ge(m_add, GROUPS)
            pe.wait_ge(q_x, 1)
            for n in range(-2, BLOCKS):
                if n + 2 < BLOCKS:
                    m = n + 2
                    r = rows(m)
                    after(pe, q_ev, m - 1)
                    for j in range(2):
                        last = nc.tensor.transpose(ps[m % 2][:, j * P:j * P + r],
                                                   agg[0:r, m * MSG + j * P:m * MSG + (j + 1) * P], ident[0:r, 0:r])
                    last.then_inc(q_t, 1)
                if 0 <= n + 1 < BLOCKS:
                    m = n + 1
                    r = rows(m)
                    bank = ps[2 + m % 2]
                    pe.wait_ge(q_ev, m + 1)
                    after(pe, q_act, m - 1)
                    mm(bank[:, 0:r], os_t[0:2 * HID, :], agg_t[0:2 * HID, m % 2, 0, 0:r], start=True, stop=True)
                    for c in (1, 0, 2):
                        h = slice(2 * HID * (1 - c % 2), 2 * HID * (2 - c % 2))
                        to = bank if c % 2 else ps[6 + m % 2]
                        last = mm(to[:, (c + 1) * P:(c + 1) * P + r], ov_t[h, :], agg_t[h, m % 2, (c + 1) // 2, 0:r],
                                  start=True, stop=True)
                    last.then_inc(q_o, 1)
                if n >= 0:
                    r = rows(n)
                    bank = ps[4 + n % 2]
                    pe.wait_ge(q_ok, n + 1)
                    after(pe, q_x, n)
                    mm(bank[0:r, 0:P], sv_t[:, n % 2, 0, 0:r], qs_t, start=True, stop=True)
                    for c in range(3):
                        last = mm(bank[0:r, (c + 1) * P:(c + 2) * P], sv_t[:, n % 2, c + 1, 0:r], qv_t,
                                  start=True, stop=True)
                    last.then_inc(q_pe, 1)
            for lay in range(2):
                for n in range(BLOCKS):
                    if lay == 0:
                        pe.wait_ge(ln_h, 3 * BLOCKS + n + 1)
                        if n == 0:
                            pe.wait_ge(q_act, BLOCKS)
                            pe.wait_ge(q_x, BLOCKS + 1)
                    else:
                        pe.wait_ge(act_h, BLOCKS + n + 1)
                    transpose_block(n)
                pe.wait_ge(adj_ok, 2)
                aggregate(ln_h if lay == 0 else act_h, 3 * BLOCKS if lay == 0 else BLOCKS)
                pe.wait_ge(ld_w3 if lay == 0 else ld_w4, 64 if lay == 0 else 32)
                for n in range(BLOCKS):
                    aggregated(n)
                    product(n, gt, wa)
                    product(n, ht, wb)

        @block.vector
        def _(dve):
            v = nc.vector
            n_v = Count()

            def layernorm(k, src_t, ready, scale=None):
                at_stat, at_std = {}, {}

                def stats(i):
                    if i < BLOCKS:
                        ready(i)
                        v.bn_stats(stat6[0:rows(i), i, :], src_t[0:rows(i), i, :]).then_inc(dve_o, n_v.up())
                        at_stat[i] = n_v.n
                    if 1 <= i < BLOCKS + 1:
                        n, r = i - 1, rows(i - 1)
                        dve.wait_ge(dve_o, at_stat[n])
                        v.bn_aggr(mv[0:r, n, :], stat6[0:r, n, :]).then_inc(ln_stat, 1)

                if scale:
                    scale()
                for i in range(BLOCKS + 3):
                    stats(i)
                    if 2 <= i < BLOCKS + 2:
                        n, r = i - 2, rows(i - 2)
                        dve.wait_ge(ln_std, BLOCKS * k + n + 1)
                        v.reciprocal(rstd[0:r, n:n + 1], std[0:r, n:n + 1]).then_inc(dve_o, n_v.up())
                        if scale:
                            dve.wait_ge(dve_o, n_v.n)
                            v.tensor_tensor(rstd[0:r, n:n + 1], rstd[0:r, n:n + 1], dis[0:r, n:n + 1], ALU.mult)\
                                .then_inc(dve_o, n_v.up())
                        at_std[n] = n_v.n
                    if i >= 3:
                        n, r = i - 3, rows(i - 3)
                        dve.wait_ge(dve_o, at_std[n])
                        v.tensor_scalar(nmr[0:r, n:n + 1], mv[0:r, n, 0:1], rstd[0:r, n:n + 1], -1.0,
                                        ALU.mult, ALU.mult).then_inc(ln_rs, 1)

            dve.wait_ge(const, 1)
            v.tensor_scalar(ident[:, :], col_id[:, :], pid[:, :], None, ALU.is_equal)
            v.tensor_scalar(below[:, :], col_id[:, :], pid[:, :], None, ALU.is_gt).then_inc(const, 1)
            v.tensor_scalar(pid_i[:, 1:2], pid_i[:, 0:1], RELS - 1, None, ALU.bitwise_and).then_inc(dve_o, n_v.up())
            dve.wait_ge(dve_o, n_v.n)
            v.tensor_copy(rel_id[:, :], pid_i[:, 1:2]).then_inc(dve_o, n_v.up())
            dve.wait_ge(dve_o, n_v.n)
            dve.wait_ge(ld_tab, 48)
            v.tensor_scalar(win_f[0:1, :], dst_i[0:1, :], 0.0, float(DSTP - WIN), ALU.max, ALU.min).then_inc(win_out, 1)
            v.tensor_scalar(win_i[0:1, :], dst_i[0:1, :], 0.0, float(DSTP - WIN), ALU.max, ALU.min)
            v.tensor_scalar(tmp_i[:, :], src_i[:, :], P - 1, None, ALU.bitwise_and).then_inc(dve_o, n_v.up())
            dve.wait_ge(dve_o, n_v.n)
            v.tensor_copy(srclo[:, :], tmp_i[:, :])
            layernorm(0, x_in, lambda n: dve.wait_ge(ld_x[0 if n < 4 else 1 if n < 9 else 2], 16))
            v.tensor_scalar(tmp_i[:, :], src_i[:, :], 7, None, ALU.logical_shift_right).then_inc(dve_o, n_v.up())
            dve.wait_ge(win_pe, 1)
            v.tensor_tensor(tmp_a[:, :], dst_i[:, :], ps[5][:, 0:CHUNKS], ALU.subtract).then_inc(dve_o, n_v.up())
            dve.wait_ge(dve_o, n_v.n)
            v.tensor_scalar(offs[:, :], tmp_a[:, :], -1.0, float(WIN), ALU.max, ALU.min)
            v.tensor_scalar(tmp_b[:, :], tmp_a[:, :], 0.0, None, ALU.is_ge).then_inc(dve_o, n_v.up())
            dve.wait_ge(dve_o, n_v.n)
            v.scalar_tensor_tensor(tmp_b[:, :], tmp_a[:, :], WIN - 0.5, tmp_b[:, :], ALU.is_lt, ALU.mult)\
                .then_inc(dve_o, n_v.up())
            dve.wait_ge(dve_o, n_v.n)
            v.tensor_reduce(inside[:, :], tmp_b[:, :], mybir.AxisListType.X, ALU.add).then_inc(cnt_in, 1)
            v.scalar_tensor_tensor(tmp_a[:, :], tmp_a[:, :], float(BLOCKS), tmp_i[:, :], ALU.mult, ALU.add)\
                .then_inc(dve_o, n_v.up())
            dve.wait_ge(dve_o, n_v.n)
            v.tensor_scalar(acol[:, :], tmp_a[:, :], -1.0, float(AWIN), ALU.max, ALU.min)
            dve.wait_ge(cnt_pe, 1)
            v.tensor_scalar(fits[0:1, 0:1], ps[6][0:1, 0:1], EDGES - 0.5, None, ALU.is_ge).then_inc(fit_ok, 1)
            dve.wait_ge(ld_wc, 16 * QUAD)
            v.tensor_copy(wc_part[:, 0, :], wc_blk[:, :]).then_inc(dve_o, n_v.up())
            dve.wait_ge(dve_o, n_v.n)
            v.tensor_tensor(wc_blk[:, :], wc_blk[:, :], wc_part[:, 0, :], ALU.subtract).then_inc(dve_o, n_v.up())
            dve.wait_ge(dve_o, n_v.n)
            v.tensor_copy(wc_part[:, 1, :], wc_blk[:, :]).then_inc(dve_o, n_v.up())
            dve.wait_ge(dve_o, n_v.n)
            v.tensor_tensor(wc_part[:, 2, :], wc_blk[:, :], wc_part[:, 1, :], ALU.subtract)
            for j in range(SLICES + 1):
                if j < SLICES:
                    dve.wait_ge(ld_et[j % 4], 16 * QUAD * (j // 4 + 1))
                    if j >= 2:
                        dve.wait_ge(coef_pe, j - 1)
                    v.tensor_scalar(et_1[:, j % 2, :], et_i[:, j % 4, :], rel_id[:, :], None, ALU.is_equal)\
                        .then_inc(et_hot, 1)
                if j:
                    c = slice((j - 1) * ETS * QUAD, j * ETS * QUAD)
                    dve.wait_ge(coef_pe, j)
                    v.tensor_tensor(coef[:, c, :],
                                    ps[(j - 1) % 5][:, 0:ETS * QUAD * BASES].rearrange("p (t b) -> p t b", b=BASES),
                                    norm_f[:, c].unsqueeze(2).broadcast_to([P, ETS * QUAD, BASES]), ALU.mult)\
                        .then_inc(coef_ok, 1)

            def load4(ap, most):
                return nc.values_load_multi_w_load_instructions(
                    ap, engines=[mybir.EngineType.DVE], min_val=0, max_val=most,
                    skip_runtime_bounds_check_because="clamped or counted on the chip")[1]

            def make_hit(g, par):
                v.tensor_tensor(hit[:, par, :, :], iota_w[:, :].unsqueeze(1).broadcast_to([P, QUAD, WIN]),
                                offs[:, bass.ds(g * QUAD, QUAD)].unsqueeze(2).broadcast_to([P, QUAD, WIN]),
                                ALU.is_equal).then_inc(hit_ok, 1)

            def make_spread(g, par):
                dve.wait_ge(hit_ok, g + 1)
                v.tensor_tensor(spread[:, par, :, :, :],
                                hit[:, par, :, :].unsqueeze(2).broadcast_to([P, QUAD, BASES, WIN]),
                                coef[:, bass.ds(g * QUAD, QUAD), :].unsqueeze(3).broadcast_to([P, QUAD, BASES, WIN]),
                                ALU.mult).then_inc(spread_ok, 1)

            def add_chunk(t, bank, w):
                dve.wait_ge(z_pe, t + 1)
                dve.wait_ge(z_add, t + 1)
                zw = z[:, :, :, bass.ds(w, WIN)]
                v.tensor_tensor(zw, zw, bank[:, :].rearrange("p (k b d) -> p k b d", k=KIN, b=BASES), ALU.add)\
                    .then_inc(z_add, 1)

            def add_quad(g, par, further, chunks=QUAD):
                w = load4(win_i[0:1, bass.ds(g * QUAD, QUAD)], DSTP - WIN)
                for q in range(chunks):
                    if q == 3 and further:
                        dve.wait_ge(z_pe, g * QUAD + QUAD)
                        make_spread(g + 2, par)
                    add_chunk(g * QUAD + q, ps[par * QUAD + q], w[q])
                    if q == 0 and further:
                        make_hit(g + 2, par)

            dve.wait_ge(coef_ok, SLICES)
            for par in range(2):
                make_hit(par, par)
            dve.wait_ge(z_zero, 3)
            dve.wait_ge(z_zero_a, 1)
            dve.wait_ge(fit_ok, 1)
            fit = dve.value_load(fits[0:1, 0:1], min_val=0, max_val=1)
            with dve.If(fit == 1):
                v.memset(turn[:, 0:1], 0.0).then_inc(z_add, 1)
                for par in range(2):
                    make_spread(par, par)
                with dve.Fori(0, FULL_QUADS // 2 - 1) as i:
                    for par in range(2):
                        add_quad(i * 2 + par, par, True)
                add_quad(FULL_QUADS - 2, 0, True)
                add_quad(FULL_QUADS - 1, 1, False)
                add_quad(FULL_QUADS, 0, False, REST)
                dve.wait_ge(z_add, REAL_CHUNKS + 1)
            with dve.Else():
                v.memset(turn[:, 0:1], 0.0).then_inc(g_add, 1)
                with dve.Fori(0, REAL_CHUNKS) as c:
                    v.tensor_scalar(one_off[:, 0:1], dst_i[:, bass.ds(c, 1)], 0.0, None, ALU.add).then_inc(g_o, 1)
                    with dve.Fori(0, WINDOWS) as k:
                        dve.wait_ge(g_o, c * (1 + 2 * WINDOWS) + k * 2 + 1)
                        v.tensor_scalar(hit[:, 0, 0, :], iota_w[:, :], one_off[:, 0:1], None, ALU.is_equal).then_inc(g_o, 1)
                        dve.wait_ge(g_o, c * (1 + 2 * WINDOWS) + k * 2 + 2)
                        v.tensor_scalar(one_off[:, 0:1], one_off[:, 0:1], -float(WIN), None, ALU.add).then_inc(g_o, 1)
                        v.tensor_tensor(spread[:, 0, 0, :, :],
                                        hit[:, 0, 0, :].unsqueeze(1).broadcast_to([P, BASES, WIN]),
                                        coef[:, bass.ds(c, 1), :].rearrange("p t b -> p (t b)").unsqueeze(2)
                                        .broadcast_to([P, BASES, WIN]), ALU.mult).then_inc(g_spread, 1)
                        dve.wait_ge(g_pe, c * WINDOWS + k + 1)
                        dve.wait_ge(g_add, c * WINDOWS + k + 1)
                        zw = z[:, :, :, bass.ds(k * WIN, WIN)]
                        v.tensor_tensor(zw, zw, ps[0][:, :].rearrange("p (k b d) -> p k b d", k=KIN, b=BASES), ALU.add)\
                            .then_inc(g_add, 1)
                dve.wait_ge(g_add, REAL_CHUNKS * WINDOWS + 1)
            v.memset(start_k[:, 0:1], 0.0).then_inc(edges_done, 1)

            v.tensor_scalar(blk_i, src_i[:, :], 7, None, ALU.logical_shift_right).then_inc(dve_o, n_v.up())
            dve.wait_ge(dve_o, n_v.n)
            v.tensor_copy(blk_f, blk_i).then_inc(dve_o, n_v.up())
            dve.wait_ge(dve_o, n_v.n)
            v.memset(blk_f[:, REAL_CHUNKS:CHUNKS], -1.0)
            v.memset(blk_f[TAIL:P, REAL_CHUNKS - 1:REAL_CHUNKS], -1.0)
            v.memset(slot_f, 0.0).then_inc(dve_o, n_v.up())
            for k in range(BLOCKS):
                dve.wait_ge(dve_o, n_v.n)
                v.tensor_scalar(in_blk, blk_f, float(k), None, ALU.is_equal).then_inc(in_ok, 1)
                dve.wait_ge(rank_pe, k + 1)
                v.tensor_tensor_scan(run_sum, ones[:, 0:1].to_broadcast([P, CHUNKS]), ps[6][:, 0:CHUNKS],
                                     start_k[:, k:k + 1], ALU.mult, ALU.add).then_inc(dve_o, n_v.up())
                dve.wait_ge(dve_o, n_v.n)
                v.tensor_scalar(sized_i[:, 0:1], run_sum[:, CHUNKS - 1:CHUNKS], GROUP - 1.0, None, ALU.add)\
                    .then_inc(dve_o, n_v.up())
                v.tensor_tensor(place, run_sum, ps[6][:, 0:CHUNKS], ALU.subtract).then_inc(dve_o, n_v.up())
                dve.wait_ge(dve_o, n_v.n - 1)
                v.tensor_scalar(sized_i[:, 1:2], sized_i[:, 0:1], 8, 8, ALU.logical_shift_right, ALU.logical_shift_left)\
                    .then_inc(dve_o, n_v.up())
                dve.wait_ge(dve_o, n_v.n - 1)
                v.tensor_tensor(place, place, ps[5][:, 0:CHUNKS], ALU.add).then_inc(dve_o, n_v.up())
                dve.wait_ge(dve_o, n_v.n - 1)
                v.tensor_copy(start_k[:, k + 1:k + 2], sized_i[:, 1:2]).then_inc(dve_o, n_v.up())
                dve.wait_ge(dve_o, n_v.n - 1)
                v.tensor_tensor(place, place, in_blk, ALU.mult).then_inc(dve_o, n_v.up())
                dve.wait_ge(dve_o, n_v.n)
                v.tensor_tensor(slot_f, slot_f, place, ALU.add).then_inc(dve_o, n_v.up())
            dve.wait_ge(dve_o, n_v.n)
            v.tensor_copy(slot_i[:, :], slot_f).then_inc(rank_ok, 1)

            def make_hot(t, slot):
                v.tensor_scalar(hot_s[:, slot, :], iota_a[:, 0:P], srclo[:, bass.ds(t, 1)], None, ALU.is_equal)
                v.tensor_scalar(hot_d[:, slot, :], iota_a[:, :], acol[:, bass.ds(t, 1)], None, ALU.is_equal)\
                    .then_inc(hot_ok, 1)

            def count_quad(g, further=QUAD, chunks=QUAD):
                w = load4(win_i[0:1, bass.ds(g * QUAD, QUAD)], DSTP - WIN)
                for q in range(chunks):
                    t = g * QUAD + q
                    dve.wait_ge(a_pe, t + 1)
                    dve.wait_ge(a_add, t + 1)
                    cw = cnt[:, :, bass.ds(w[q], WIN)]
                    v.tensor_tensor(cw, cw, ps[5 + q % 2][:, 0:AWIN].rearrange("p (d s) -> p s d", s=BLOCKS), ALU.add)\
                        .then_inc(a_add, 1)
                    if q < further:
                        make_hot(t + QUAD, q)

            def take_half(half):
                dve.wait_ge(half_pe, half + 1)
                for j in range(HALF):
                    m = half * HALF + j
                    r = rows(m)
                    if half == 0:
                        dve.wait_ge(ld_xl if j < 2 else ld_xz, 32 if j < 2 else 48)
                        x_at, to = x_low[j][0:r, :], x_low[j][0:r, :]
                    else:
                        dve.wait_ge(ld_xh, 16 * HALF)
                        x_at, to = x_high[j][0:r, :], xs[0:r, m, :]
                    v.tensor_tensor(to, ps[j][0:r, :], x_at, ALU.add).then_inc(o_free, 1)
                dve.wait_ge(ld_bias, 16)
                for j in range(HALF):
                    m = half * HALF + j
                    r = rows(m)
                    to = x_low[j][0:r, :] if half == 0 else xs[0:r, m, :]
                    dve.wait_ge(o_free, m + 1)
                    v.tensor_tensor(to, to, bias0[0:r, :], ALU.add).then_inc(o_done, 1)

            def sum_blocks():
                for i, (a, b) in enumerate(((0, HALF * P), (HALF * P, NODES))):
                    last = v.tensor_reduce(deg_part[i], cnt[:, :, a:b].rearrange("p s d -> p d s"),
                                           mybir.AxisListType.X, ALU.add)
                last.then_inc(cnt_done, 1)

            dve.wait_ge(cnt_zero, 1)
            with dve.If(fit == 1):
                v.memset(turn[:, 1:2], 0.0).then_inc(a_add, 1)
                for t in range(QUAD):
                    make_hot(t, t)
                with dve.Fori(0, LOW_COUNTS // QUAD) as g:
                    count_quad(g)
                take_half(0)
                with dve.Fori(LOW_COUNTS // QUAD, FULL_QUADS - 1) as g:
                    count_quad(g)
                count_quad(FULL_QUADS - 1, REST)
                count_quad(FULL_QUADS, 0, REST)
                dve.wait_ge(a_add, REAL_CHUNKS + 1)
                sum_blocks()
                take_half(1)
            with dve.Else():
                v.memset(turn[:, 1:2], 0.0).then_inc(ga_add, 1)
                with dve.Fori(0, REAL_CHUNKS) as c:
                    v.tensor_scalar(hot_s[:, 0, :], iota_a[:, 0:P], srclo[:, bass.ds(c, 1)], None, ALU.is_equal)
                    v.tensor_scalar(sized_i[:, 0:1], src_i[:, bass.ds(c, 1)], 7, None, ALU.logical_shift_right)
                    v.tensor_scalar(one_off[:, 1:2], dst_i[:, bass.ds(c, 1)], float(BLOCKS), None, ALU.mult)\
                        .then_inc(ga_o, 1)
                    dve.wait_ge(ga_o, c * (2 + WINDOWS) + 1)
                    v.tensor_tensor(one_off[:, 0:1], one_off[:, 1:2], sized_i[:, 0:1], ALU.add).then_inc(ga_o, 1)
                    with dve.Fori(0, WINDOWS) as k:
                        dve.wait_ge(ga_o, c * (2 + WINDOWS) + k + 2)
                        v.tensor_scalar(hot_d[:, 0, :], iota_a[:, :], one_off[:, 0:1], None, ALU.is_equal)\
                            .then_inc(ga_hot, 1)
                        dve.wait_ge(ga_pe, c * WINDOWS + k + 1)
                        v.tensor_scalar(one_off[:, 0:1], one_off[:, 0:1], -float(AWIN), None, ALU.add).then_inc(ga_o, 1)
                        dve.wait_ge(ga_add, c * WINDOWS + k + 1)
                        cw = cnt[:, :, bass.ds(k * WIN, WIN)]
                        v.tensor_tensor(cw, cw, ps[5][:, 0:AWIN].rearrange("p (d s) -> p s d", s=BLOCKS), ALU.add)\
                            .then_inc(ga_add, 1)
                dve.wait_ge(ga_add, REAL_CHUNKS * WINDOWS + 1)
                take_half(0)
                sum_blocks()
                take_half(1)

            def degrees():
                v.memset(deg[:, :], 0.0).then_inc(dve_o, n_v.up())
                dve.wait_ge(dve_o, n_v.n)
                dve.wait_ge(deg_pe, 1)
                v.tensor_copy(deg[:, 0:BLOCKS - 1], ps[7][:, 0:BLOCKS - 1])
                v.tensor_copy(deg[0:LAST, BLOCKS - 1:BLOCKS], ps[7][0:LAST, BLOCKS - 1:BLOCKS]).then_inc(deg_ok, 1)
                dve.wait_ge(deg_ok, 1)
                v.tensor_scalar(inv[:, :], deg[:, :], 1.0, None, ALU.max).then_inc(dve_o, n_v.up())
                dve.wait_ge(dve_o, n_v.n)
                v.reciprocal(inv[:, :], inv[:, :])
                dve.wait_ge(deg_sq, 1)
                v.reciprocal(dis[:, :], dis[:, :]).then_inc(dve_o, n_v.up())
                dve.wait_ge(dve_o, n_v.n)

            def x_ready(n):
                if n < HALF:
                    dve.wait_ge(o_done, BLOCKS)
                    v.tensor_copy(adj[:, n, :], cnt[:, n, 0:NODES]).then_inc(dve_o, n_v.up())
                    dve.wait_ge(ld_x1, 16)

            layernorm(1, xs, x_ready, degrees)
            dve.wait_ge(dve_o, n_v.n)
            for n in range(BLOCKS):
                r = rows(n)
                if n >= 5:
                    dve.wait_ge(adj_act, n - 4)
                diag = adj[0:r, n, n * P:n * P + r]
                last = v.tensor_tensor(diag, diag, ident[0:r, 0:r], ALU.add)
            last.then_inc(adj_ok, 1)
            v.memset(seg_g[:, :], float(GROUP)).then_inc(dve_o, n_v.up())
            dve.wait_ge(dve_o, n_v.n)
            v.tensor_tensor_scan(seg_f[:, :], ones[0:1, 0:1].to_broadcast([1, GROUPS]), seg_g[:, :], -float(GROUP),
                                 ALU.mult, ALU.add).then_inc(dve_o, n_v.up())
            dve.wait_ge(dve_o, n_v.n)
            v.memset(seg_g[:, :], 0.0).then_inc(dve_o, n_v.up())
            for k in range(1, BLOCKS):
                dve.wait_ge(dve_o, n_v.n)
                v.scalar_tensor_tensor(seg_g[:, :], seg_f[:, :], start_k[0:1, k:k + 1], seg_g[:, :], ALU.is_ge, ALU.add)\
                    .then_inc(dve_o, n_v.up())
            dve.wait_ge(dve_o, n_v.n)
            v.tensor_scalar(seg_i[:, :], seg_g[:, :], float(MSG), None, ALU.mult).then_inc(dve_o, n_v.up())

            def add_bias(k):
                for n in range(BLOCKS):
                    r = rows(n)
                    dve.wait_ge(ln_h, BLOCKS * k + n + 1)
                    v.tensor_tensor(xs[0:r, n, :], xs[0:r, n, :], b_b[0:r, :], ALU.add).then_inc(dve_o, n_v.up())
                dve.wait_ge(dve_o, n_v.n)

            def lin_bank(unit):
                dve.wait_ge(lin_pe, unit + 1)
                return ps[4 + unit % 4]

            dve.wait_ge(ld_w12, 64)
            add_bias(1)
            for n in range(BLOCKS):
                r = rows(n)
                bank = lin_bank(n)
                if n >= 2:
                    dve.wait_ge(act_h, n - 1)
                v.scalar_tensor_tensor(low[0:r, n % 2, :], bank[0:r, :], dis[0:r, n:n + 1], b_a[0:r, :], ALU.mult, ALU.add)\
                    .then_inc(lin_ok, 1)
            for n in range(BLOCKS):
                r = rows(n)
                bank = lin_bank(BLOCKS + n)
                v.scalar_tensor_tensor(xs[0:r, n, :], bank[0:r, :], dis[0:r, n:n + 1], xs[0:r, n, :], ALU.mult, ALU.add)\
                    .then_inc(lin_ok, 1)
            layernorm(2, xs, lambda n: dve.wait_ge(lin_ok, BLOCKS + n + 1))

            dve.wait_ge(ld_mp, 16 * 15)
            b2, left = b2_f[:, 0, :], b2_f[:, 1, :]
            v.tensor_copy(b2_p[:, 0, :], b2).then_inc(dve_o, n_v.up())
            dve.wait_ge(dve_o, n_v.n)
            v.tensor_tensor(left, b2, b2_p[:, 0, :], ALU.subtract).then_inc(dve_o, n_v.up())
            dve.wait_ge(dve_o, n_v.n)
            v.tensor_copy(b2_p[:, 1, :], left).then_inc(dve_o, n_v.up())
            dve.wait_ge(dve_o, n_v.n)
            v.tensor_tensor(b2_p[:, 2, :], left, b2_p[:, 1, :], ALU.subtract).then_inc(dve_o, n_v.up())
            dve.wait_ge(dve_o, n_v.n)
            v.tensor_scalar(b2_r[:, :], b2_p[:, 0, :], ident[0:3, 0:1], None, ALU.mult).then_inc(dve_o, n_v.up())
            for i in (1, 2):
                dve.wait_ge(dve_o, n_v.n)
                v.scalar_tensor_tensor(b2_r[:, :], b2_p[:, i, :], ident[0:3, i:i + 1], b2_r[:, :], ALU.mult, ALU.add)\
                    .then_inc(dve_o, n_v.up())
            dve.wait_ge(dve_o, n_v.n)
            dve.sem_inc(pre_ok, 1)
            v.memset(agg, 0.0).then_inc(pre_ok, 1)
            for n in range(BLOCKS):
                diag = adj[0:rows(n), n, n * P:n * P + rows(n)]
                last = v.tensor_tensor(diag, diag, ident[0:rows(n), 0:rows(n)], ALU.subtract)
            last.then_inc(adj_ok, 1)

            def slot_words(rpar, a, b):
                return at[:, rpar, :, :, :].rearrange("p s g (c w) -> p (s g c) w", c=2)[:, :, a:b]

            def messages(st, r, par, s8):
                us = u[:, s8 % QUAD, :, 0:HID]
                uv = u[:, s8 % QUAD, :, HID:P].rearrange("p c (y f) -> p c y f", y=3)
                out_v = msg[:, par, :, 2 * HID:MSG].rearrange("p c (y f) -> p c y f", y=3)
                w = ps[par][:, :].rearrange("p (c w) -> p c w", c=QUAD)
                rpar, q = s8 // QUAD % 2, s8 % QUAD * QUAD
                y = yr[:, rpar, q:q + QUAD, 1:4].unsqueeze(3).broadcast_to([P, QUAD, 3, HID])
                dve.wait_ge(y_ok, r + 1)
                after(dve, m_ok, st)
                dve.wait_ge(u_in[s8 % QUAD], 64 * (s8 // QUAD) + 64 + (st - s8) * 16)
                v.tensor_tensor(vy[:, :, :, :], uv, y, ALU.mult).then_inc(v_ok, 1)
                after(dve, m_pe, 2 * st - 2)
                v.tensor_tensor(hot[:, par, :, :], iota_h[:, :].unsqueeze(1).broadcast_to([P, QUAD, P]),
                                src_of[:, rpar, q:q + QUAD, :].broadcast_to([P, QUAD, P]), ALU.is_equal)
                dve.wait_ge(v_ok, st * 4 + 1)
                v.tensor_tensor(v_sum[:, :, :], vy[:, :, 0, :], vy[:, :, 1, :], ALU.add).then_inc(v_ok, 1)
                dve.wait_ge(p_ok, st + 1)
                v.tensor_tensor(out_v[:, :, :, HID:2 * HID],
                                py[:, par, :, HID:2 * HID].unsqueeze(2).broadcast_to([P, QUAD, 3, HID]), uv, ALU.mult)
                dve.wait_ge(v_ok, st * 4 + 2)
                v.tensor_tensor(v_sum[:, :, :], v_sum[:, :, :], vy[:, :, 2, :], ALU.add).then_inc(v_ok, 1)
                v.tensor_tensor(sw[:, :, :], w[:, :, 3 * HID:P], us, ALU.mult).then_inc(v_ok, 1)
                v.tensor_tensor(msg[:, par, :, 0:HID], py[:, par, :, 0:HID], us, ALU.mult)
                dve.wait_ge(v_ok, st * 4 + 3)
                v.tensor_tensor(msg[:, par, :, HID:2 * HID], w[:, :, 2 * HID:3 * HID], v_sum[:, :, :], ALU.mult)
                dve.wait_ge(v_ok, st * 4 + 4)
                v.tensor_tensor(out_v[:, :, :, 0:HID], sw[:, :, :].unsqueeze(2).broadcast_to([P, QUAD, 3, HID]), y,
                                ALU.mult).then_inc(m_ok, 1)

            seg_at = {}

            def message(st, r, par, s8):
                rpar = (s8 // QUAD + 1) % 2
                if more(r + 1) and s8 % QUAD == 3:
                    dve.wait_ge(h_act, r + 2)
                    after(dve, w_pe, st - QUAD + 1)
                    v.scalar_tensor_tensor(hid[:, rpar, :], soft[:, 0, :], -LOG2, soft[:, 1, :],
                                           ALU.add, ALU.add).then_inc(h_ok, 1)
                if valid(st):
                    messages(st, r, par, s8)
                if more(r + 1) and s8 % QUAD == 0:
                    dve.wait_ge(ld_at[rpar], loaded(r + 1, rpar))
                    if not isinstance(r, int) or r >= 1:
                        dve.wait_ge(m_ok, st)
                        dve.wait_ge(p_ok, st)
                    v.tensor_copy(src_of[:, rpar, :, :], slot_words(rpar, SRCC, SRCC + 1))
                    v.tensor_tensor(yr[:, rpar, :, :], slot_words(rpar, YCOL, YCOL + 4),
                                    slot_words(rpar, RCUT, RCUT + 1).broadcast_to([P, QUAD * QUAD, 4]), ALU.mult)\
                        .then_inc(y_ok, 1)
                if s8 % 2 == 0 and valid(st):
                    if isinstance(st, int) and st == 0:
                        seg_at[0] = [None, None] + list(load4(seg_i[0:1, 0:QUAD], MSG * (BLOCKS - 1))[0:2])
                    else:
                        seg_at[0] = load4(seg_i[0:1, bass.ds(st * 2 - 2, QUAD)], MSG * (BLOCKS - 1))
                if not (isinstance(st, int) and st < 1):
                    add_groups(st - 1, 1 - par, seg_at[0][0:2] if par == 0 else seg_at[0][2:4])

            def add_groups(st, par, seg):
                for g in range(2):
                    dve.wait_ge(m_pe, 2 * st + g + 1)
                    dve.wait_ge(m_add, 2 * st + g)
                    a = agg[:, bass.ds(seg[g], MSG)]
                    v.tensor_tensor(a, a, ps[4 + 2 * par + g][:, 0:MSG], ALU.add).then_inc(m_add, 1)

            message_steps(dve, message)
            add_groups(STEPS - 1, (STEPS - 1) % 2, load4(seg_i[0:1, GROUPS - QUAD:GROUPS], MSG * (BLOCKS - 1))[2:4])
            dve.wait_ge(ld_mq, 16 * 5)
            v.tensor_scalar(os_t[HID:2 * HID, :], os_t[HID:2 * HID, :], IS3, None, ALU.mult).then_inc(q_x, 1)
            for n in range(-1, BLOCKS):
                if n + 1 < BLOCKS:
                    m, r = n + 1, rows(n + 1)
                    dve.wait_ge(q_act, m + 1)
                    after(dve, q_pe, m - 1)
                    v.scalar_tensor_tensor(sv_t[:, m % 2, 0, 0:r], ssp[:, m % 2, 0, 0:r], -LOG2, ssp[:, m % 2, 2, 0:r],
                                           ALU.add, ALU.add).then_inc(q_ok, 1)
                if n >= 0:
                    r = rows(n)
                    bank = ps[4 + n % 2]
                    dve.wait_ge(q_pe, n + 1)
                    v.scalar_tensor_tensor(xs[0:r, n, 0:P], bank[0:r, 0:P], P ** -0.5, xs[0:r, n, 0:P],
                                           ALU.mult, ALU.add)
                    xv = xs[0:r, n, P:FEAT].rearrange("p (d c) -> p c d", c=3)
                    v.scalar_tensor_tensor(xv, bank[0:r, P:FEAT].rearrange("p (c d) -> p c d", c=3), P ** -0.5, xv,
                                           ALU.mult, ALU.add).then_inc(q_x, 1)
            layernorm(3, xs, lambda n: dve.wait_ge(q_x, n + 2))
            dve.wait_ge(ld_w3, 64)
            add_bias(3)
            for lay in range(2):
                for n in range(BLOCKS):
                    r = rows(n)
                    unit = 2 * BLOCKS * (lay + 1) + 2 * n
                    bank = lin_bank(unit)
                    if lay == 0 and n >= 2:
                        dve.wait_ge(act_h, BLOCKS + n - 1)
                    if lay == 1:
                        dve.wait_ge(act_h, 2 * BLOCKS)
                        after(dve, st_o[n % 2], 16 * (n // 2))
                    v.scalar_tensor_tensor(low[0:r, n % 2, :], bank[0:r, :], inv[0:r, n:n + 1],
                                           b_a[0:r, :] if lay == 0 else xs[0:r, n, :], ALU.mult, ALU.add)\
                        .then_inc(lin_ok, 1)
                    bank = lin_bank(unit + 1)
                    dve.wait_ge(lin_ok, unit + 1)
                    v.tensor_tensor(low[0:r, n % 2, :], low[0:r, n % 2, :], bank[0:r, :], ALU.add).then_inc(lin_ok, 1)


def kernel(x, src, dst, edge_attr_20, edge_attr_4, edge_type_32, edge_weight, edge_weight1, L0_gnn_bases, L0_gnn_w_comp,
           L0_gnn_h_bias, L1_gnn_W1, L1_gnn_b1, L1_gnn_W2, L1_gnn_b2, L2_gnn_w_in2f_s, L2_gnn_w_in2f_v, L2_gnn_W1,
           L2_gnn_b1, L2_gnn_W2, L2_gnn_b2, L2_gnn_w_f2o1_s, L2_gnn_w_f2o1_v, L2_gnn_w_f2o2_s, L2_gnn_w_f2o2_v,
           L3_gnn_label, L3_gnn_W1_l, L3_gnn_W1_r, L3_gnn_b1, L3_gnn_W2_l, L3_gnn_W2_r, L3_gnn_b2):
    import numpy as np
    import concourse.bacc as bacc
    from concourse.bass_utils import run_bass_kernel_spmd

    def by_chunks(a, fill=0):
        a = np.asarray(a).reshape(EDGES, -1)
        pad = np.full((CHUNKS * P - EDGES, a.shape[1]), fill, a.dtype)
        return np.concatenate([a, pad]).reshape(CHUNKS, P, -1).transpose(1, 0, 2)

    order = [0, 3, 1, 2]
    f32 = np.float32
    etype = by_chunks(edge_type_32)[:, :, 0].reshape(P, CHUNKS // QUAD, QUAD).transpose(2, 1, 0).reshape(QUAD, -1)
    words = [np.asarray(edge_attr_20), np.asarray(edge_attr_4), np.asarray(edge_weight).reshape(EDGES, 1),
             np.zeros((EDGES, ROW - RCUT - 1), f32)]
    arrays = dict(
        src=by_chunks(src)[:, :, 0], dst=by_chunks(dst, PADDST)[:, :, 0], etype=etype,
        norm=by_chunks(edge_weight1)[:, :, 0], attr=by_chunks(np.concatenate(words, axis=1)), x=x,
        bases=L0_gnn_bases, w_comp=L0_gnn_w_comp, h_bias=np.asarray(L0_gnn_h_bias).reshape(1, FEAT),
        g_w1=L1_gnn_W1, g_b1=np.asarray(L1_gnn_b1).reshape(1, FEAT), g_w2=L1_gnn_W2,
        g_b2=np.asarray(L1_gnn_b2).reshape(1, FEAT),
        m_ws=L2_gnn_w_in2f_s, m_wv=L2_gnn_w_in2f_v, m_w1=L2_gnn_W1, m_b1=np.asarray(L2_gnn_b1).reshape(HID, 1),
        m_w2=np.asarray(L2_gnn_W2).reshape(HID, HID, 6)[:, :, order].transpose(0, 2, 1).reshape(HID, 4 * HID),
        m_b2=np.asarray(L2_gnn_b2).reshape(HID, 6)[:, order].T.reshape(1, 4 * HID),
        m_os=L2_gnn_w_f2o1_s, m_ov=L2_gnn_w_f2o1_v, m_qs=L2_gnn_w_f2o2_s, m_qv=L2_gnn_w_f2o2_v,
        s_w1l=np.asarray(L3_gnn_W1_l).T, s_w1r=np.asarray(L3_gnn_W1_r).T, s_b1=np.asarray(L3_gnn_b1).reshape(1, FEAT),
        s_w2l=np.asarray(L3_gnn_W2_l).T, s_w2r=np.asarray(L3_gnn_W2_r).T, s_b2=np.asarray(L3_gnn_b2).reshape(1, FEAT))

    nc = bacc.Bacc("TRN2", target_bir_lowering=False, num_devices=1)
    ins, args = {}, {}
    for name, a in arrays.items():
        a = np.ascontiguousarray(a)
        ins[f"in_{name}_dram"] = a
        args[name] = nc.dram_tensor(f"in_{name}_dram", a.shape, mybir.dt.from_np(a.dtype), kind="ExternalInput").ap()
    args["out"] = nc.dram_tensor("out_0_dram", (NODES, FEAT), mybir.dt.float32, kind="ExternalOutput").ap()
    graph_layers(nc, **args)
    r = run_bass_kernel_spmd(nc, [ins], core_ids=[0])
    return r.results[0]["out_0_dram"]
```
